# Optimizing a Trainium2 kernel written in Bass

```python
import numpy as np
import jax
import jax.numpy as jnp

def _softmax(x, axis=-1):
    return jax.nn.softmax(x, axis=axis)

def _gelu(x):
    return jax.nn.gelu(x, approximate=True)

def _silu(x):
    return jax.nn.silu(x)

def _sigmoid(x):
    return jax.nn.sigmoid(x)

def _layernorm(x, axis=-1, eps=1e-05):
    m = jnp.mean(x, axis=axis, keepdims=True)
    v = jnp.var(x, axis=axis, keepdims=True)
    return (x - m) / jnp.sqrt(v + eps)

def _scatter_add(tgt, idx, src, axis=0):
    return tgt.at[idx].add(src)

def _segment_sum(src, seg, n):
    return jax.ops.segment_sum(src, seg, n)
kernel_name = 'mk_decoder_postln_d1_seqx_r8_ee9f3c'

def setup_inputs(seed: int=0):
    np.random.seed(seed)
    _w = jnp.asarray

    def _rec_inputs():
        import jax
        import jax.numpy as jnp
        _rk = jax.random.key(seed)
        x = 7.22e-05 + 1 * jax.random.normal(jax.random.fold_in(_rk, 1), (16, 64, 256), jnp.float32)
        _lenS = 64 - jax.random.randint(jax.random.fold_in(_rk, 7), (16,), 0, max(1, 64 // 4) + 1, jnp.int32)
        _lenS2 = 64 - jax.random.randint(jax.random.fold_in(_rk, 8), (16,), 0, max(1, 64 // 4) + 1, jnp.int32)
        _ctx_512P = jax.random.normal(jax.random.fold_in(_rk, 11), (16, 16, 64), jnp.float32)
        _ctx_512c = jax.random.dirichlet(jax.random.fold_in(_rk, 511), 0.3 * jnp.ones((16,), jnp.float32), (16, 64))
        _ctx_512t = jnp.einsum('bsk,bkd->bsd', _ctx_512c, _ctx_512P)
        _ctx_512t = _ctx_512t * jax.lax.rsqrt(jnp.mean(jnp.square(_ctx_512t)) + 1e-12) * 0.953939
        ctx_512 = -0.000514642 + 1.00011 * (_ctx_512t + 0.3 * jax.random.normal(jax.random.fold_in(_rk, 611), (16, 64, 64), jnp.float32))
        return (x, ctx_512)
    x, ctx_512 = _rec_inputs()

    def _L0_attn_setup():
        import jax, jax.numpy as jnp
        import numpy as np
        B, T, E, H, L = (1, 256, 256, 16, 64)
        D = E // H
        RA_WINDOW = 64
        RA_ALPHA = 0.5
        key = jax.random.key(seed)
        ks = jax.random.split(key, 7)

        def w(k, shape, fan_in):
            return jax.random.normal(k, shape, dtype=jnp.float32) / np.sqrt(fan_in)
        return {'hidden_states': jax.random.normal(ks[0], (B, T, E), dtype=jnp.float32), 'w_q': w(ks[1], (E, E), E), 'w_k_down': w(ks[2], (L, E), E), 'w_v_down': w(ks[3], (L, E), E), 'q_to_latent': w(ks[4], (H, D, L), D), 'v_up': w(ks[5], (H, L, D), L), 'w_out': w(ks[6], (E, E), E)}
    _L0_attn_all = _L0_attn_setup()
    _L0_attn_in = {k: v for k, v in _L0_attn_all.items() if k in ('w_q', 'w_k_down', 'w_v_down', 'q_to_latent', 'v_up', 'w_out')}
    del _L0_attn_all

    def _L0_xattn_setup():
        import jax, jax.numpy as jnp
        import numpy as np
        import math
        NUM_Q_HEADS = 32
        NUM_KV_HEADS = 8
        key = jax.random.key(seed)
        k1, k2, k3 = jax.random.split(key, 3)
        B, S, E = (2, 256, 256)
        kv_E = NUM_KV_HEADS * (E // NUM_Q_HEADS)
        q = jax.random.normal(k1, (B, S, E), dtype=jnp.float32)
        k = jax.random.normal(k2, (B, S, kv_E), dtype=jnp.float32)
        v = jax.random.normal(k3, (B, S, kv_E), dtype=jnp.float32)
        return {'q': q, 'k': k, 'v': v}
    _L0_xattn_all = _L0_xattn_setup()
    _L0_xattn_in = {k: v for k, v in _L0_xattn_all.items() if k in ()}
    del _L0_xattn_all

    def _L0_ffn_setup():
        import jax, jax.numpy as jnp
        import numpy as np
        SEQ, BS, D, F, E = (128, 2, 256, 256, 8)
        key = jax.random.key(seed)
        ks = jax.random.split(key, 8)
        s = 0.02
        return {'hidden_states': jax.random.normal(ks[0], (SEQ, BS, D), jnp.float32), 'router_w': jax.random.normal(ks[1], (D, E), jnp.float32) * s, 'gate_w': jax.random.normal(ks[2], (E, D, F), jnp.float32) * s, 'up_w': jax.random.normal(ks[3], (E, D, F), jnp.float32) * s, 'down_w': jax.random.normal(ks[4], (E, F, D), jnp.float32) * s, 'shared_gate_w': jax.random.normal(ks[5], (D, F), jnp.float32) * s, 'shared_up_w': jax.random.normal(ks[6], (D, F), jnp.float32) * s, 'shared_down_w': jax.random.normal(ks[7], (F, D), jnp.float32) * s}
    _L0_ffn_all = _L0_ffn_setup()
    _L0_ffn_in = {k: v for k, v in _L0_ffn_all.items() if k in ('router_w', 'gate_w', 'up_w', 'down_w', 'shared_gate_w', 'shared_up_w', 'shared_down_w')}
    del _L0_ffn_all
    return {'x': x, 'ctx_512': ctx_512, 'L0_attn_w_q': _L0_attn_in['w_q'], 'L0_attn_w_k_down': _L0_attn_in['w_k_down'], 'L0_attn_w_v_down': _L0_attn_in['w_v_down'], 'L0_attn_q_to_latent': _L0_attn_in['q_to_latent'], 'L0_attn_v_up': _L0_attn_in['v_up'], 'L0_attn_w_out': _L0_attn_in['w_out'], 'L0_ffn_router_w': _L0_ffn_in['router_w'], 'L0_ffn_gate_w': _L0_ffn_in['gate_w'], 'L0_ffn_up_w': _L0_ffn_in['up_w'], 'L0_ffn_down_w': _L0_ffn_in['down_w'], 'L0_ffn_shared_gate_w': _L0_ffn_in['shared_gate_w'], 'L0_ffn_shared_up_w': _L0_ffn_in['shared_up_w'], 'L0_ffn_shared_down_w': _L0_ffn_in['shared_down_w']}

def reference(x, ctx_512, L0_attn_w_q, L0_attn_w_k_down, L0_attn_w_v_down, L0_attn_q_to_latent, L0_attn_v_up, L0_attn_w_out, L0_ffn_router_w, L0_ffn_gate_w, L0_ffn_up_w, L0_ffn_down_w, L0_ffn_shared_gate_w, L0_ffn_shared_up_w, L0_ffn_shared_down_w):
    import jax
    import jax.numpy as jnp

    def _L0_attn_ref(hidden_states, w_q, w_k_down, w_v_down, q_to_latent, v_up, w_out):
        import jax, jax.numpy as jnp
        import numpy as np
        B, T, E, H, L = (1, 256, 256, 16, 64)
        D = E // H
        RA_WINDOW = 64
        RA_ALPHA = 0.5
        b, t, e = hidden_states.shape
        h, d, l = q_to_latent.shape
        Q = (hidden_states @ w_q.T).reshape(b, t, h, d)
        latent_k = hidden_states @ w_k_down.T
        latent_v = hidden_states @ w_v_down.T
        q_latent = jnp.einsum('bthd,hdl->bthl', Q, q_to_latent)
        raw = jnp.einsum('bthl,bsl->bhts', q_latent, latent_k) / jnp.sqrt(jnp.float32(l))
        pos = jnp.arange(t)
        causal = pos[None, :] <= pos[:, None]
        band = jnp.abs(pos[:, None] - pos[None, :]) < RA_WINDOW
        logits = jnp.where(causal, raw, -jnp.inf)
        logits = jnp.where(band & causal, raw * (1.0 + RA_ALPHA), logits)
        attn = jax.nn.softmax(logits, axis=-1)
        V = jnp.einsum('btl,hld->bthd', latent_v, v_up)
        ctx = jnp.einsum('bhts,bshd->bthd', attn, V)
        out = ctx.reshape(b, t, h * d) @ w_out.T
        return out

    def _L0_xattn_ref(q, k, v):
        import jax, jax.numpy as jnp
        import numpy as np
        import math
        NUM_Q_HEADS = 32
        NUM_KV_HEADS = 8
        B, S, E = q.shape
        H, KV = (NUM_Q_HEADS, NUM_KV_HEADS)
        D = E // H
        G = H // KV
        scale = math.sqrt(D)
        qh = q.reshape(B, S, KV, G, D).transpose(0, 2, 3, 1, 4)
        kh = k.reshape(B, S, KV, D).transpose(0, 2, 1, 3)
        vh = v.reshape(B, S, KV, D).transpose(0, 2, 1, 3)
        scores = jnp.einsum('bkgsd,bktd->bkgst', qh, kh) / scale
        weights = jax.nn.softmax(scores, axis=-1)
        out = jnp.einsum('bkgst,bktd->bkgsd', weights, vh)
        return out.transpose(0, 3, 1, 2, 4).reshape(B, S, E)

    def _L0_ffn_ref(hidden_states, router_w, gate_w, up_w, down_w, shared_gate_w, shared_up_w, shared_down_w):
        import jax, jax.numpy as jnp
        import numpy as np
        SEQ, BS, D, F, E = (128, 2, 256, 256, 8)
        S, B, Dm = hidden_states.shape
        x = hidden_states.reshape(-1, Dm)
        logits = x @ router_w
        expert_idx = jnp.argmax(logits, axis=-1)
        score = jax.nn.sigmoid(jnp.max(logits, axis=-1))
        xs = x * score[:, None]
        n_experts = router_w.shape[1]
        out = jnp.zeros_like(x)
        for e in range(n_experts):
            m = (expert_idx == e)[:, None]
            xe = jnp.where(m, xs, 0.0)
            h = jax.nn.silu(xe @ gate_w[e]) * (xe @ up_w[e])
            out = out + jnp.where(m, h @ down_w[e], 0.0)
        shared = jax.nn.silu(x @ shared_gate_w) * (x @ shared_up_w) @ shared_down_w
        return (out + shared).reshape(S, B, Dm)
    x = _layernorm(x + _L0_attn_ref(x, L0_attn_w_q, L0_attn_w_k_down, L0_attn_w_v_down, L0_attn_q_to_latent, L0_attn_v_up, L0_attn_w_out), axis=-1)
    x = _layernorm(x + _L0_xattn_ref(x, ctx_512, ctx_512), axis=-1)
    x = _layernorm(x + _L0_ffn_ref(x, L0_ffn_router_w, L0_ffn_gate_w, L0_ffn_up_w, L0_ffn_down_w, L0_ffn_shared_gate_w, L0_ffn_shared_up_w, L0_ffn_shared_down_w), axis=-1)
    return x

_drawn_inputs = setup_inputs


def setup_inputs(seed=0):
    import zlib

    import numpy as np

    out = dict(_drawn_inputs(seed))
    spreads = {}
    factors = {'L0_ffn_router_w': 8.0,
     'L0_ffn_gate_w': 8.0,
     'L0_ffn_up_w': 8.0,
     'L0_ffn_down_w': 8.0,
     'L0_ffn_shared_gate_w': 3.168,
     'L0_ffn_shared_up_w': 3.237,
     'L0_ffn_shared_down_w': 3.115}
    for name, (base, spread) in spreads.items():
        noise = np.random.default_rng([zlib.crc32(name.encode()), seed]).standard_normal(out[name].shape)
        drawn = base * np.exp(spread * noise) if base else spread * noise
        out[name] = jnp.asarray(drawn.astype(out[name].dtype))
    for name, factor in factors.items():
        out[name] = (out[name] * factor).astype(out[name].dtype)
    return out
```

```python
from contextlib import ExitStack

import concourse.bass as bass
from concourse import mybir

F32 = mybir.dt.float32
BF16 = mybir.dt.bfloat16
U32 = mybir.dt.uint32
I32 = mybir.dt.int32
ALU = mybir.AluOpType
ACT = mybir.ActivationFunctionType
AX = mybir.AxisListType.X

P = 128
B, T, E = 16, 64, 256
TILES = B * T // P
H, D = 16, 16
L = 64
KC = E // P
HG = P // D
XKV, XG, XD = 8, 4, 8
CX = XKV * XD
NE = 8
F = 256
WROW = KC * 2 * F + KC * E
BLOCKS = (B * T - NE) // P + NE
SLOTS = BLOCKS * P
SELF_SCALE = 1.5 / float(L) ** 0.5
CROSS_SCALE = 1.0 / float(XD) ** 0.5
EPS = 1e-5

C_IDENT, C_EXPERT, C_STEP, C_BEFORE, C_BLOCK, C_EPS, C_POW = 0, 128, 136, 144, 208, 223, 224
C_WIDTH = 225
M_IDENT, M_CAUSAL, M_RANK, M_ONES = 0, 128, 640, 768
M_WIDTH = 896


def decoder_layer(nc, x, xT, ctx_k, ctx_v, w_q, w_small, w_out, w_ffn, router, consts, masks, out):
    with ExitStack() as stack:
        def sb(name, shape, dt=F32):
            return stack.enter_context(nc.sbuf_tensor(name, shape, dt))

        def bank(name, n=1):
            return stack.enter_context(nc.psum_tensor(name, [P, 512 * n], F32))

        def sem(name):
            return stack.enter_context(nc.semaphore(name))

        cst = sb("cst", [P, C_WIDTH])
        msk = sb("msk", [P, M_WIDTH], BF16)
        wq = sb("wq", [P, KC, E])
        wsm = sb("wsm", [L, 4, E])
        wk = sb("wk", [P, KC, E])
        wv = sb("wv", [P, KC, 2, P])
        wo = sb("wo", [P, KC, E])
        wrt = sb("wrt", [P, KC, NE])
        wff = sb("wff", [P, NE + 1, WROW])
        x_all = sb("x_all", [P, TILES, E])
        z_all = sb("z_all", [P, TILES, E])
        kx = sb("kx", [P, TILES, 2, 512])
        vnat = sb("vnat", [P, B, CX])
        onehot = sb("onehot", [P, TILES, NE], BF16)
        xTt = sb("xTt", [P, 2, KC, P])
        qT = sb("qT", [P, 2, 2, P])
        kT = sb("kT", [P, 2, 2, 2, T])
        kbd = sb("kbd", [P, 2, 2, 2, 512])
        vbd = sb("vbd", [P, 2, 2, 8, 32])
        m1 = sb("m1", [P, H])
        p1 = sb("p1", [P, H, T])
        msk32 = p1[:, :, :].rearrange("p h s -> p (h s)")[:, 0:M_WIDTH]
        l1 = sb("l1", [P, H])
        r1 = sb("r1", [P, H])
        p1n = sb("p1n", [P, H, T])
        p1T = sb("p1T", [P, 8, P])
        cT = sb("cT", [P, 2, P])
        res1 = sb("res1", [P, E])
        st1 = sb("st1", [P, 6])
        mv1 = sb("mv1", [P, 2])
        va1 = sb("va1", [P, 1])
        rs1 = sb("rs1", [P, 1])
        x1 = sb("x1", [P, 2, E])
        qx = sb("qx", [P, XG, T])
        m2 = sb("m2", [P, 2, 2 * XKV])
        p2 = sb("p2", [P, 2, 2 * XKV, T])
        p2T = sb("p2T", [P, 2, 4, 2, P])
        vx = sb("vx", [P, 2, 2, 4, 2, 16])
        oT = sb("oT", [P, XG, 2, T])
        rl2 = sb("rl2", [P, XG, XKV])
        a2 = sb("a2", [P, E])
        res2 = sb("res2", [P, E])
        st2 = sb("st2", [P, 6])
        mv2 = sb("mv2", [P, 2])
        va2 = sb("va2", [P, 1])
        rs2 = sb("rs2", [P, 1])
        x2 = sb("x2", [P, 2, E])
        x2T = sb("x2T", [P, KC, P])
        sg = sb("sg", [P, F])
        sd = sb("sd", [P, F])
        sh = sb("sh", [P, F])
        hid = sb("hid", [P, F])
        hT = sb("hT", [P, KC, P])
        top = sb("top", [P, 8])
        topi = sb("topi", [P, 8], U32)
        topf = sb("topf", [P, 1])
        sc_e = sb("sc_e", [P, 1])
        sc_d = sb("sc_d", [P, 1])
        score = sb("score", [P, 1])
        xs = sb("xs", [P, TILES, E])
        tot = sb("tot", [P, TILES, NE])
        base = sb("base", [P, TILES, NE])
        cnt = sb("cnt", [P, NE])
        over = sb("over", [P, NE, 8])
        nb = sb("nb", [P, NE])
        bef = sb("bef", [P, NE, NE])
        bst = sb("bst", [P, NE])
        bend = sb("bend", [P, NE])
        bst128 = sb("bst128", [P, NE])
        slot1 = sb("slot1", [P, TILES, NE])
        slot2 = sb("slot2", [P, TILES, NE])
        slot3 = sb("slot3", [P, TILES, NE])
        posf = sb("posf", [P, TILES])
        pos = sb("pos", [P, TILES], U32)
        ebc = sb("ebc", [P, BLOCKS, NE])
        ebf = sb("ebf", [P, BLOCKS])
        ebm = sb("ebm", [P, BLOCKS])
        ebi = sb("ebi", [P, BLOCKS], I32)
        room = kx[:, :, :, :].rearrange("p t s n -> p (t s n)")
        xe, eg, ed, er, eh, ehid, ye = (room[:, 2 * E * i:2 * E * i + 2 * E].rearrange("p (a n) -> p a n", a=2)
                                        for i in range(7))
        xeT, ehT = (room[:, 2 * E * i:2 * E * i + 2 * E].rearrange("p (a k n) -> p a k n", a=2, k=KC)
                    for i in range(7, 9))
        zero = sb("zero", [P, E])
        yg, res3 = xs, z_all
        st3 = sb("st3", [P, TILES, 6])
        mv3 = sb("mv3", [P, TILES, 2])
        va3 = sb("va3", [P, TILES])
        rs3 = sb("rs3", [P, TILES])
        fin = x_all

        xs_sorted = nc.dram_tensor("xs_sorted", (SLOTS, E), F32, kind="Internal").ap()
        ys_sorted = nc.dram_tensor("ys_sorted", (SLOTS, E), F32, kind="Internal").ap()

        def sorted_rows(rows, j):
            return rows.rearrange("(j p) c -> j p c", p=P)[j]

        sA = bank("sA", 2)
        sB = bank("sB", 2)
        tp = [bank("tp0"), bank("tp1")]
        b6 = bank("b6")
        b7 = bank("b7")

        ident = cst[:, C_IDENT:C_IDENT + P]

        def flat(ap):
            names = "abcdef"[:len(ap.shape) - 1]
            return ap.rearrange(f"p {' '.join(names)} -> p ({' '.join(names)})")

        d_first, d_small, d_x, d_kx, d_vn, d_ffn, d_shared = (sem(s) for s in (
            "d_first", "d_small", "d_x", "d_kx", "d_vn", "d_ffn", "d_shared"))
        d_zero = sem("d_zero")
        d_xT = [sem("d_xT0"), sem("d_xT1")]
        d_kbd = [sem("d_kbd0"), sem("d_kbd1")]
        d_disp = sem("d_disp")
        passed = sem("passed")
        d_xe = [sem(f"d_xe{i}") for i in range(2)]
        d_ye = [sem(f"d_ye{i}") for i in range(2)]
        d_yg = [sem(f"d_yg{i}") for i in range(TILES)]
        d_out = sem("d_out")
        kbd_zeroed, vbd_zeroed, kx_zeroed, vx_zeroed, zero_ok = (sem(s) for s in (
            "kbd_zeroed", "vbd_zeroed", "kx_zeroed", "vx_zeroed", "zero_ok"))
        fuse_mm, fuse_cp, msk_ok = sem("fuse_mm"), sem("fuse_cp"), sem("msk_ok")
        names = """qk_mm v_mm q_cp k_cp v_cp s1_mm m1_ok sub1 exp1 sum1 rec1 nrm1
        pt1a_mm pt1b_mm pt1a_cp pt1b_cp c_mm c_cp o1_mm res1_ok st1_ok mv1_ok va1_ok rs1_ok x1_ok
        qx_mm qx_cp s2a_mm s2b_mm m2a m2b sub2a sub2b exp2a exp2b pt2_mm0 pt2_mm1 pt2_mm2 pt2_mm3
        pt2_cp0 pt2_cp1 pt2_cp2 pt2_cp3 vx_half vx_ok o2_mm o2_cp ot_mm rl2_ok a2_ok res2_ok st2_ok mv2_ok
        va2_ok rs2_ok x2_ok x2T_mm x2T_cp gu_mm lg_mm sg_ok sd_ok sr_ok sh_ok hid_ok hT_mm hT_cp
        dn_mm z_ok top_ok topi_ok topf_ok hot_ok sce_ok scd_ok score_ok xs_ok
        rank_mm xeT_mm xeT_cp egu_mm eg_ok ed_ok er_ok eh_ok ehid_ok ehT_mm ehT_cp edn_mm ye_ok
        route ebi_ok pos_ok res3_ok st3_ok mv3_ok va3_ok rs3_ok fin_ok""".split()
        S = {name: sem(name) for name in names}

        def after(eng, name, count):
            if isinstance(count, int) and count <= 0:
                return
            eng.wait_ge(S[name], count)

        def after_alone(eng, name, count):
            after(eng, name, count)
            eng.sem_inc(passed, 1)

        def steps(eng, step):
            def peeled(n):
                step(n, n // 2, n % 2, n < TILES, 1 <= n <= TILES, n >= 2, n + 1 < TILES)

            peeled(0)
            peeled(1)
            with eng.Fori(1, TILES // 2 - 1) as it:
                for p in range(2):
                    step(2 * it + p, it, p, True, True, True, True)
            for n in range(TILES - 2, TILES + 2):
                peeled(n)

        def expert_turns(eng, turn):
            turn(0)
            with eng.Fori(1, BLOCKS // 2) as it:
                turn(it)

        block = stack.enter_context(nc.Block())

        @block.sync
        def _(sp):
            sp.dma_start(wsm[:, :, :], w_small).then_inc(d_small, 16)
            sp.dma_start(xTt[:, 0, :, :], xT[0]).then_inc(d_xT[0], 16)
            sp.dma_start(wq[:, :, :], w_q).then_inc(d_first, 16)
            sp.dma_start(msk32, masks).then_inc(d_first, 16)
            sp.dma_start(cst[:, :], consts).then_inc(d_first, 16)
            sp.dma_start(xTt[:, 1, :, :], xT[1]).then_inc(d_xT[1], 16)
            sp.dma_start(x_all[:, :, :], x.rearrange("t p c -> p t c")).then_inc(d_x, 16)
            sp.dma_start(wo[:, :, :], w_out).then_inc(d_first, 16)
            sp.dma_start(wrt[:, :, :], router).then_inc(d_first, 16)
            for half in range(2):
                sp.dma_start(vnat[64 * half:64 * half + 64, :, :], ctx_v.rearrange("b s c -> s b c")).then_inc(d_vn, 16)

            def diagonal(p):
                for h in range(HG):
                    sp.dma_start(kbd[D * h:D * h + D, p, :, :, T * h:T * h + T],
                                 kT[D * h:D * h + D, p, :, :, :]).then_inc(d_kbd[p], 16)

            def load(n, half, p, *_):
                after_alone(sp, "k_cp", n + 1)
                after_alone(sp, "s1_mm", n - 1)
                diagonal(p)

            sp.wait_ge(kbd_zeroed, 1)
            load(0, 0, 0)
            sp.dma_start(xTt[:, 0, :, :], xT[2]).then_inc(d_xT[0], 16)
            sp.wait_ge(kx_zeroed, 1)
            for b in range(2):
                for kv in range(XKV):
                    r = CX * b + XD * kv
                    sp.dma_start(kx[r:r + XD, :, b, T * kv:T * kv + T], ctx_k[b, kv]).then_inc(d_kx, 16)
            load(1, 0, 1)
            sp.dma_start(xTt[:, 1, :, :], xT[3]).then_inc(d_xT[1], 16)
            sp.dma_start(wff[:, NE, :], w_ffn[NE]).then_inc(d_shared, 16)
            with sp.Fori(1, TILES // 2 - 1) as it:
                for p in range(2):
                    load(2 * it + p, it, p)
                    sp.dma_start(xTt[:, p, :, :], xT[2 * it + p + 2]).then_inc(d_xT[p], 16)
            for n in range(TILES - 2, TILES):
                load(n, n // 2, n % 2)

            sp.wait_ge(d_disp, 16 * TILES)

            def load_block(j, p):
                after_alone(sp, "xeT_mm", j - 1)
                sp.dma_start(xe[:, p, :], sorted_rows(xs_sorted, j)).then_inc(d_xe[p], 16)

            def store_block(j, p):
                after_alone(sp, "ye_ok", j + 1)
                sp.dma_start(sorted_rows(ys_sorted, j), ye[:, p, :]).then_inc(d_ye[p], 16)

            load_block(0, 0)
            load_block(1, 1)
            with sp.Fori(1, BLOCKS // 2) as it:
                for p in range(2):
                    load_block(2 * it + p, p)
                    store_block(2 * it + p - 2, p)
            load_block(BLOCKS - 1, 0)
            for j in range(BLOCKS - 3, BLOCKS):
                store_block(j, j % 2)
            for t in range(TILES):
                after(sp, "fin_ok", t + 1)
                sp.dma_start(out[t], fin[:, t, :]).then_inc(d_out, 16)
            sp.wait_ge(d_out, 16 * TILES)

        @block.gpsimd
        def _(pool):
            pool.memset(kbd[:, :, :, :, :], 0.0).then_inc(kbd_zeroed, 1)
            pool.memset(vx[:, :, :, :, :, :], 0.0).then_inc(vx_zeroed, 1)
            pool.wait_ge(vx_zeroed, 1)
            for kv in range(2):
                pool.memset(vx[64 * kv:64 * kv + 64, :, :, :, kv, XD:XD + 1], 1.0).then_inc(vx_zeroed, 1)
                pool.wait_ge(vx_zeroed, 2 + kv)
            pool.memset(kx[:, :, :, :], 0.0).then_inc(kx_zeroed, 1)
            pool.wait_ge(zero_ok, 1)
            for j in range(BLOCKS):
                pool.dma_start(xs_sorted[P * j:P * j + P, :], zero[:, :]).then_inc(d_zero, 16)
            for e in range(NE):
                pool.dma_start(wff[:, e, :], w_ffn[e]).then_inc(d_ffn, 16)
            pool.wait_ge(d_vn, 32)
            pool.wait_ge(vx_zeroed, 3)
            pool.wait_ge(d_first, 80)

            def step(n, half, p, do_self, do_cross, do_ffn, do_proj):
                q = 1 - p
                if do_cross:
                    for kv in range(2):
                        rows = slice(64 * kv, 64 * kv + 64)
                        src = vnat[rows, bass.ds(2 * (n - 1), 2), :].rearrange("p b (k v d) -> p b k v d", k=4, v=2)
                        name = ("vx_half", "vx_ok")[kv]
                        pool.tensor_copy(vx[rows, q, :, :, kv, 0:XD], src[:, :, :, kv, :]).then_inc(S[name], 1)
                        after(pool, name, n)
                if do_self:
                    after(pool, "rec1", n + 1)
                    after(pool, "pt1b_mm", n)
                    pool.tensor_tensor(p1n[:, :, :], p1[:, :, :],
                                       r1[:, :].unsqueeze(2).to_broadcast([P, H, T]), ALU.mult).then_inc(S["nrm1"], 1)
                if do_ffn:
                    after(pool, "score_ok", n - 1)
                    pool.tensor_tensor(xs[:, n - 2, :], x2[:, p, :],
                                       score[:, 0:1].to_broadcast([P, E]), ALU.mult).then_inc(S["xs_ok"], 1)
                if do_self:
                    after(pool, "va1_ok", n + 1)
                    pool.tensor_tensor(rs1[:, :], va1[:, :], cst[:, C_POW:C_POW + 1], ALU.pow).then_inc(S["rs1_ok"], 1)
                if do_cross:
                    after(pool, "va2_ok", n)
                    pool.tensor_tensor(rs2[:, :], va2[:, :], cst[:, C_POW:C_POW + 1], ALU.pow).then_inc(S["rs2_ok"], 1)

            steps(pool, step)

            after(pool, "xs_ok", TILES)
            after(pool, "pos_ok", 1)
            pool.wait_ge(d_zero, 16 * BLOCKS)
            for t in range(TILES):
                pool.indirect_dma_start(xs_sorted, bass.IndirectOffsetOnAxis(pos[:, t:t + 1], 0),
                                        xs[:, t, :], None).then_inc(d_disp, 16)
            pool.wait_ge(d_ye[0], 16 * ((BLOCKS + 1) // 2))
            pool.wait_ge(d_ye[1], 16 * (BLOCKS // 2))
            for t in range(TILES):
                pool.indirect_dma_start(yg[:, t, :], None, ys_sorted,
                                        bass.IndirectOffsetOnAxis(pos[:, t:t + 1], 0)).then_inc(d_yg[t], 16)
            for t in range(TILES):
                after(pool, "va3_ok", t + 1)
                pool.tensor_tensor(rs3[:, t:t + 1], va3[:, t:t + 1], cst[:, C_POW:C_POW + 1], ALU.pow).then_inc(S["rs3_ok"], 1)

        @block.tensor
        def _(pe):
            def mm(o, lhsT, rhs, start=True, stop=True, **k):
                return pe.matmul(o, lhsT, rhs, start=start, stop=stop, **k)

            pe.wait_ge(d_small, 16)
            for w in range(2):
                for k in range(KC):
                    last = mm(sB[:, 512 * w + E * k:512 * w + E * k + E], wsm[:, w, P * k:P * k + P], wsm[:, 2 + w, :])
            last.then_inc(fuse_mm, 1)
            pe.wait_ge(fuse_cp, 2)
            pe.wait_ge(d_first, 80)
            pe.wait_ge(msk_ok, 1)

            def values(t, half, p):
                pe.wait_ge(d_xT[p], 16 * half + 16)
                for par in range(2):
                    for s in range(2):
                        for k in range(KC):
                            last = mm(b7[64 * par:64 * par + 64, P * s:P * s + P], xTt[:, p, k, T * s:T * s + T],
                                      wv[:, k, par, :], start=(k == 0), stop=(k == KC - 1))
                last.then_inc(S["v_mm"], 1)

            def queries_keys(t, p):
                for w, weight in enumerate((wq, wk)):
                    for g in range(2):
                        for k in range(KC):
                            last = mm(b6[:, P * (2 * w + g):P * (2 * w + g) + P], weight[:, k, P * g:P * g + P],
                                      xTt[:, p, k, :], start=(k == 0), stop=(k == KC - 1))
                last.then_inc(S["qk_mm"], 1)

            values(0, 0, 0)
            queries_keys(0, 0)

            def step(n, half, p, do_self, do_cross, do_ffn, do_proj):
                q = 1 - p
                if do_self:
                    after(pe, "k_cp", n + 1)
                    pe.wait_ge(d_kbd[p], 16 * HG * (half + 1))
                    after(pe, "sub2b", n - 1)
                    for g in range(2):
                        for s in range(2):
                            o = sA[T * s:T * s + T, 512 * g:512 * g + 512]
                            mm(o, msk[:, M_IDENT + T * s:M_IDENT + T * s + T], msk[:, M_CAUSAL:M_CAUSAL + 512], stop=False)
                            last = mm(o, qT[:, p, g, T * s:T * s + T], kbd[:, p, g, s, :], start=False)
                    last.then_inc(S["s1_mm"], 1)
                if do_cross:
                    after(pe, "x1_ok", n)
                    after(pe, "a2_ok", n - 1)
                    x1v = x1[:, q, :].rearrange("p (g c) -> p g c", g=XG)
                    for s in range(2):
                        for g in range(XG):
                            last = mm(b6[64 * s:64 * s + 64, T * g:T * g + T], x1v[:, g, :],
                                      cst[:, C_IDENT + T * s:C_IDENT + T * s + T])
                    last.then_inc(S["qx_mm"], 1)
                    after(pe, "qx_cp", n)
                    after(pe, "sub2a", n - 1)
                    if isinstance(n, int) and n == 1:
                        pe.wait_ge(d_kx, 16 * 2 * XKV)
                        pe.wait_ge(d_shared, 16)
                    for s in range(2):
                        last = mm(sB[:, 512 * s:512 * s + 512], flat(qx[:, 0:2, :]), kx[:, n - 1, s, :])
                    last.then_inc(S["s2a_mm"], 1)
                if do_ffn:
                    after(pe, "x2_ok", n - 1)
                    after(pe, "o2_cp", n - 1)
                    for k in range(KC):
                        last = pe.transpose(b7[:, P * k:P * k + P], x2[:, p, P * k:P * k + P], ident)
                    last.then_inc(S["x2T_mm"], 1)
                    after(pe, "x2T_cp", n - 1)
                    if do_cross:
                        after(pe, "qx_cp", n)
                    else:
                        after(pe, "a2_ok", n - 1)
                    for k in range(KC):
                        last = mm(b6[:, :], x2T[:, k, :], wff[:, NE, 2 * F * k:2 * F * k + 2 * F],
                                  start=(k == 0), stop=(k == KC - 1))
                    last.then_inc(S["gu_mm"], 1)
                    for k in range(KC):
                        last = mm(b7[:, 0:NE], x2T[:, k, :], wrt[:, k, :], start=(k == 0), stop=(k == KC - 1))
                    last.then_inc(S["lg_mm"], 1)
                if do_self:
                    after(pe, "nrm1", n + 1)
                    for c, bank_ in enumerate(tp):
                        after(pe, ("pt2_cp2", "pt2_cp3")[c], n - 1)
                        for i in range(4):
                            hp = 4 * c + i
                            last = pe.transpose(bank_[:, P * i:P * i + P], flat(p1n[:, 2 * hp:2 * hp + 2, :]), ident)
                        last.then_inc(S[("pt1a_mm", "pt1b_mm")[c]], 1)
                if do_cross:
                    if do_self:
                        after(pe, "sub1", n + 1)
                    else:
                        after(pe, "sub2b", n - 1)
                    for s in range(2):
                        last = mm(sA[:, 512 * s:512 * s + 512], flat(qx[:, 2:4, :]), kx[:, n - 1, s, :])
                    last.then_inc(S["s2b_mm"], 1)
                if do_self:
                    after(pe, "pt1b_cp", n + 1)
                    after(pe, "v_cp", n + 1)
                    if do_ffn:
                        after(pe, "topi_ok", n - 1)
                    for s in range(2):
                        for hp in range(8):
                            r = 32 * (hp % 4)
                            last = mm(b7[r:r + 32, P * (hp // 4) + T * s:P * (hp // 4) + T * s + T],
                                      vbd[:, p, s, hp, :], p1T[:, hp, T * s:T * s + T])
                    last.then_inc(S["c_mm"], 1)
                if do_ffn:
                    after(pe, "hid_ok", n - 1)
                    for k in range(KC):
                        last = pe.transpose(b6[:, P * k:P * k + P], hid[:, P * k:P * k + P], ident)
                    last.then_inc(S["hT_mm"], 1)
                if do_self:
                    after(pe, "c_cp", n + 1)
                    for g in range(KC):
                        last = mm(b7[:, 0:E], cT[:, g, :], wo[:, g, :], start=(g == 0), stop=(g == KC - 1))
                    last.then_inc(S["o1_mm"], 1)

                def probs(gp):
                    after(pe, ("exp2a", "exp2b")[gp], n)
                    for s in range(2):
                        if gp == 1:
                            after(pe, f"pt2_cp{s}", n)
                        elif do_self:
                            after(pe, ("pt1a_cp", "pt1b_cp")[s], n + 1)
                        else:
                            after(pe, f"pt2_cp{2 + s}", n - 1)
                        for i in range(4):
                            last = pe.transpose(tp[s][:, P * i:P * i + P],
                                                flat(p2[:, gp, XKV * s + 2 * i:XKV * s + 2 * i + 2, :]), ident)
                        last.then_inc(S[f"pt2_mm{2 * gp + s}"], 1)

                if do_cross:
                    probs(0)
                if do_ffn:
                    after(pe, "hT_cp", n - 1)
                    for k in range(KC):
                        last = mm(b6[:, 0:E], hT[:, k, :],
                                  wff[:, NE, KC * 2 * F + E * k:KC * 2 * F + E * k + E],
                                  start=(k == 0), stop=(k == KC - 1))
                    last.then_inc(S["dn_mm"], 1)
                if do_cross:
                    probs(1)
                if do_proj:
                    after(pe, "res1_ok", n + 1)
                    project_next(n, half, p, do_ffn)
                if do_cross:
                    after(pe, "pt2_cp3", n)
                    after(pe, "vx_ok", n)
                    if do_proj:
                        after(pe, "v_cp", n + 2)
                    elif do_self:
                        after(pe, "res1_ok", n + 1)
                    else:
                        after(pe, "topi_ok", n - 1)
                    for s in range(2):
                        for kp in range(4):
                            last = mm(b7[32 * kp:32 * kp + 32, 256 * s:256 * s + 256], flat(vx[:, q, s, kp, :, :]),
                                      flat(p2T[:, s, kp, :, :]))
                    last.then_inc(S["o2_mm"], 1)
                    after(pe, "o2_cp", n)
                    if do_proj:
                        after(pe, "k_cp", n + 2)
                    elif do_ffn:
                        after(pe, "z_ok", n - 1)
                    for g in range(XG):
                        last = pe.transpose(b6[:, P * g:P * g + P], flat(oT[:, g, :, :]), ident)
                    last.then_inc(S["ot_mm"], 1)

            def project_next(n, half, p, do_ffn):
                q = 1 - p
                nhalf = half + p
                values(n + 1, nhalf, q)
                if do_ffn:
                    after(pe, "z_ok", n - 1)
                queries_keys(n + 1, q)

            steps(pe, step)

            after(pe, "hot_ok", TILES)
            after(pe, "z_ok", TILES)
            hot = onehot[:, :, :].rearrange("p t e -> p (t e)")
            mm(b6[:, 0:TILES * NE], msk[:, M_RANK:M_RANK + P], hot)
            mm(b6[:, 64:64 + TILES * NE], msk[:, M_ONES:M_ONES + P], hot, skip_group_check=True).then_inc(S["rank_mm"], 1)

            pe.wait_ge(d_ffn, 16 * NE)
            after(pe, "ebi_ok", 1)

            def transpose_hidden(j, r):
                after(pe, "ehid_ok", j + 1)
                after(pe, "ehT_cp", j - 1)
                for k in range(KC):
                    last = pe.transpose(sB[:, 512 * r + P * k:512 * r + P * k + P], ehid[:, r, P * k:P * k + P], ident)
                last.then_inc(S["ehT_mm"], 1)

            def up_block(j, p, half, before_up):
                pe.wait_ge(d_xe[p], 16 * (half + 1))
                after(pe, "xeT_cp", j - 1)
                for k in range(KC):
                    last = pe.transpose(tp[p][:, P * k:P * k + P], xe[:, p, P * k:P * k + P], ident)
                last.then_inc(S["xeT_mm"], 1)
                before_up()
                after(pe, "xeT_cp", j + 1)
                after_alone(pe, "ehid_ok", j - 1)
                e = pe.value_load(ebi[0:1, bass.ds(j, 1)], min_val=0, max_val=NE - 1)
                for k in range(KC):
                    last = mm(sA[:, 512 * p:512 * p + 512], xeT[:, p, k, :],
                              flat(wff[:, bass.ds(e, 1), 2 * F * k:2 * F * k + 2 * F]), start=(k == 0), stop=(k == KC - 1))
                last.then_inc(S["egu_mm"], 1)

            def down_block(j, r):
                after(pe, "ehT_cp", j + 1)
                after_alone(pe, "ye_ok", j - 1)
                e = pe.value_load(ebi[0:1, bass.ds(j, 1)], min_val=0, max_val=NE - 1)
                for k in range(KC):
                    c = KC * 2 * F + E * k
                    last = mm((b6, b7)[r][:, 0:E], ehT[:, r, k, :], flat(wff[:, bass.ds(e, 1), c:c + E]),
                              start=(k == 0), stop=(k == KC - 1))
                last.then_inc(S["edn_mm"], 1)

            def pe_blocks(it):
                for u in range(2):
                    j, p = 2 * it + 1 + u, 1 - u
                    up_block(j, p, it + u, lambda: transpose_hidden(j - 1, 1 - p))
                    down_block(j - 1, 1 - p)

            up_block(0, 0, 0, lambda: None)
            expert_turns(pe, pe_blocks)
            transpose_hidden(BLOCKS - 1, (BLOCKS - 1) % 2)
            down_block(BLOCKS - 1, (BLOCKS - 1) % 2)

        @block.scalar
        def _(act):
            act.wait_ge(d_first, 80)
            act.copy(msk[:, :], msk32).then_inc(msk_ok, 1)
            act.wait_ge(fuse_mm, 1)
            act.copy(flat(wk[:, :, :]), sB[:, 0:512]).then_inc(fuse_cp, 1)

            def copy_qk(t, p):
                after(act, "qk_mm", t + 1)
                act.mul(flat(qT[:, p, :, :]), b6[:, 0:E], SELF_SCALE).then_inc(S["q_cp"], 1)
                act.copy(flat(kT[:, p, :, :, :]), b6[:, E:2 * E]).then_inc(S["k_cp"], 1)

            copy_qk(0, 0)

            def step(n, half, p, do_self, do_cross, do_ffn, do_proj):
                q = 1 - p
                if do_cross:
                    after(act, "qx_mm", n)
                    act.mul(flat(qx[:, :, :]), b6[:, 0:E], CROSS_SCALE).then_inc(S["qx_cp"], 1)
                if do_ffn:
                    after(act, "x2T_mm", n - 1)
                    act.copy(flat(x2T[:, :, :]), b7[:, 0:E]).then_inc(S["x2T_cp"], 1)
                if do_self:
                    after(act, "sub1", n + 1)
                    act.activation(p1[:, :, :], p1[:, :, :], ACT.Exp).then_inc(S["exp1"], 1)
                if do_ffn:
                    after(act, "gu_mm", n - 1)
                    act.activation(sg[:, :], b6[:, 0:F], ACT.Exp, scale=-1.0).then_inc(S["sg_ok"], 1)
                    after(act, "top_ok", n - 1)
                    act.activation(sc_e[:, :], top[:, 0:1], ACT.Exp, scale=-1.0).then_inc(S["sce_ok"], 1)
                if do_cross:
                    after(act, "sub2a", n)
                    act.activation(p2[:, 0, :, :], p2[:, 0, :, :], ACT.Exp).then_inc(S["exp2a"], 1)
                if do_self:
                    after(act, "pt1a_mm", n + 1)
                    after(act, "c_mm", n)
                    act.copy(flat(p1T[:, 0:4, :]), tp[0][:, :]).then_inc(S["pt1a_cp"], 1)
                    after(act, "pt1b_mm", n + 1)
                    act.copy(flat(p1T[:, 4:8, :]), tp[1][:, :]).then_inc(S["pt1b_cp"], 1)
                if do_cross:
                    after(act, "sub2b", n)
                    act.activation(p2[:, 1, :, :], p2[:, 1, :, :], ACT.Exp).then_inc(S["exp2b"], 1)
                if do_self:
                    after(act, "c_mm", n + 1)
                    act.copy(flat(cT[:, :, :]), b7[:, 0:E]).then_inc(S["c_cp"], 1)
                if do_ffn:
                    after(act, "hT_mm", n - 1)
                    act.copy(flat(hT[:, :, :]), b6[:, 0:E]).then_inc(S["hT_cp"], 1)
                if do_cross:
                    after(act, "o2_mm", n - 1)
                    for gp in range(2):
                        for s in range(2):
                            after(act, f"pt2_mm{2 * gp + s}", n)
                            act.copy(p2T[:, s, :, gp, :], tp[s][:, :].rearrange("p (k t) -> p k t", k=4)).then_inc(
                                S[f"pt2_cp{2 * gp + s}"], 1)
                if do_proj:
                    copy_qk(n + 1, q)
                if do_cross:
                    after(act, "o2_mm", n)
                    act.copy(oT[:, :, :, :], b7[:, :].rearrange("p (s g t) -> p g s t", s=2, g=XG)).then_inc(S["o2_cp"], 1)

            steps(act, step)

            def copy_rows(j, p):
                after(act, "xeT_mm", j + 1)
                after(act, "egu_mm", j - 1)
                act.copy(flat(xeT[:, p, :, :]), tp[p][:, 0:E]).then_inc(S["xeT_cp"], 1)

            def copy_hidden(j, r):
                after(act, "ehT_mm", j + 1)
                after(act, "edn_mm", j - 1)
                act.copy(flat(ehT[:, r, :, :]), sB[:, 512 * r:512 * r + E]).then_inc(S["ehT_cp"], 1)

            def exp_gate(j, p):
                after(act, "egu_mm", j + 1)
                after(act, "ed_ok", j - 1)
                act.activation(eg[:, p, :], sA[:, 512 * p:512 * p + F], ACT.Exp, scale=-1.0).then_inc(S["eg_ok"], 1)

            def copy_result(j, r, stored):
                after(act, "edn_mm", j + 1)
                if not isinstance(stored, int) or stored > 0:
                    act.wait_ge(d_ye[r], 16 * stored)
                act.copy(ye[:, r, :], (b6, b7)[r][:, 0:E]).then_inc(S["ye_ok"], 1)

            def act_blocks(it):
                for u in range(2):
                    j, p = 2 * it + 1 + u, 1 - u
                    copy_rows(j, p)
                    copy_hidden(j - 1, 1 - p)
                    exp_gate(j, p)
                    copy_result(j - 1, 1 - p, it)

            copy_rows(0, 0)
            exp_gate(0, 0)
            expert_turns(act, act_blocks)
            copy_hidden(BLOCKS - 1, 0)
            copy_result(BLOCKS - 1, 0, BLOCKS // 2)

        @block.vector
        def _(dve):
            dve.memset(zero[:, :], 0.0).then_inc(zero_ok, 1)
            dve.memset(vbd[:, :, :, :, :], 0.0).then_inc(vbd_zeroed, 1)
            dve.wait_ge(vbd_zeroed, 1)
            dve.wait_ge(fuse_mm, 1)
            dve.tensor_copy(flat(wv[:, :, :, :]), sB[:, 512:1024]).then_inc(fuse_cp, 1)

            def copy_v(t, p):
                after(dve, "v_mm", t + 1)
                after(dve, "c_mm", t - 1)
                for par in range(2):
                    rows = slice(64 * par, 64 * par + 64)
                    last = dve.tensor_copy(vbd[rows, p, :, :, D * par:D * par + D],
                                    b7[rows, 0:E].rearrange("p (s h d) -> p s h d", s=2, h=8))
                last.then_inc(S["v_cp"], 1)

            copy_v(0, 0)
            dve.wait_ge(d_first, 80)
            dve.wait_ge(d_x, 16)

            def norm(t, src, stats, mv, va, i):
                dve.bn_stats(stats, src).then_inc(S[f"st{i}_ok"], 1)
                after_alone(dve, f"st{i}_ok", t + 1)
                dve.bn_aggr(mv, stats).then_inc(S[f"mv{i}_ok"], 1)
                after(dve, f"mv{i}_ok", t + 1)
                dve.tensor_scalar(va, mv[:, 1:2], EPS, None, ALU.add).then_inc(S[f"va{i}_ok"], 1)

            def step(n, half, p, do_self, do_cross, do_ffn, do_proj):
                q = 1 - p
                if do_self:
                    after(dve, "s1_mm", n + 1)
                    s1 = sA[:, :].rearrange("p (h s) -> p h s", h=H)
                    dve.tensor_reduce(m1[:, :], s1, AX, ALU.max).then_inc(S["m1_ok"], 1)
                    after(dve, "m1_ok", n + 1)
                    after(dve, "nrm1", n)
                    dve.tensor_tensor(p1[:, :, :], s1, m1[:, :].unsqueeze(2).to_broadcast([P, H, T]),
                                      ALU.subtract).then_inc(S["sub1"], 1)

                def cross_max(gp, s_, mm_name):
                    after(dve, mm_name, n)
                    s2 = s_[:, :].rearrange("p (k s) -> p k s", k=2 * XKV)
                    name = "ab"[gp]
                    dve.tensor_reduce(m2[:, gp, :], s2, AX, ALU.max).then_inc(S[f"m2{name}"], 1)
                    after(dve, f"m2{name}", n)
                    after(dve, f"pt2_mm{2 * gp + 1}", n - 1)
                    dve.tensor_tensor(p2[:, gp, :, :], s2, m2[:, gp, :].unsqueeze(2).to_broadcast([P, 2 * XKV, T]),
                                      ALU.subtract).then_inc(S[f"sub2{name}"], 1)

                if do_cross:
                    cross_max(0, sB, "s2a_mm")
                if do_self:
                    after(dve, "exp1", n + 1)
                    dve.tensor_reduce(l1[:, :], p1[:, :, :], AX, ALU.add).then_inc(S["sum1"], 1)
                    after(dve, "sum1", n + 1)
                    dve.reciprocal(r1[:, :], l1[:, :]).then_inc(S["rec1"], 1)
                if do_ffn:
                    after_alone(dve, "lg_mm", n - 1)
                    dve.max(top[:, :], b7[:, 0:NE]).then_inc(S["top_ok"], 1)
                    after_alone(dve, "top_ok", n - 1)
                    dve.max_index(topi[:, :], top[:, :], b7[:, 0:NE]).then_inc(S["topi_ok"], 1)
                    after(dve, "topi_ok", n - 1)
                    dve.tensor_copy(topf[:, :], topi[:, 0:1]).then_inc(S["topf_ok"], 1)
                    after(dve, "topf_ok", n - 1)
                    dve.tensor_scalar(onehot[:, n - 2, :], cst[:, C_EXPERT:C_EXPERT + NE], topf[:, 0:1], None,
                                      ALU.is_equal).then_inc(S["hot_ok"], 1)
                if do_cross:
                    cross_max(1, sA, "s2b_mm")
                if do_ffn:
                    after(dve, "sg_ok", n - 1)
                    dve.tensor_scalar(sd[:, :], sg[:, :], 1.0, None, ALU.add).then_inc(S["sd_ok"], 1)
                    after(dve, "sce_ok", n - 1)
                    dve.tensor_scalar(sc_d[:, :], sc_e[:, :], 1.0, None, ALU.add).then_inc(S["scd_ok"], 1)
                    after(dve, "sd_ok", n - 1)
                    dve.reciprocal(sh[:, :], sd[:, :]).then_inc(S["sr_ok"], 1)
                    after(dve, "scd_ok", n - 1)
                    dve.reciprocal(score[:, :], sc_d[:, :]).then_inc(S["score_ok"], 1)
                    after(dve, "sr_ok", n - 1)
                    dve.tensor_tensor(sd[:, :], b6[:, 0:F], sh[:, :], ALU.mult).then_inc(S["sh_ok"], 1)
                    after(dve, "sh_ok", n - 1)
                    dve.tensor_tensor(hid[:, :], b6[:, F:2 * F], sd[:, :], ALU.mult).then_inc(S["hid_ok"], 1)
                if do_self:
                    after(dve, "o1_mm", n + 1)
                    dve.tensor_tensor(res1[:, :], b7[:, 0:E], x_all[:, n, :], ALU.add).then_inc(S["res1_ok"], 1)
                    after(dve, "res1_ok", n + 1)
                    norm(n, res1[:, :], st1[:, :], mv1[:, :], va1[:, :], 1)
                if do_proj:
                    copy_v(n + 1, q)
                if do_self:
                    after(dve, "rs1_ok", n + 1)
                    after(dve, "res2_ok", n - 1)
                    dve.tensor_scalar(x1[:, p, :], res1[:, :], mv1[:, 0:1], rs1[:, 0:1],
                                      ALU.subtract, ALU.mult).then_inc(S["x1_ok"], 1)
                if do_ffn:
                    after(dve, "dn_mm", n - 1)
                    dve.tensor_tensor(z_all[:, n - 2, :], b6[:, 0:E], x2[:, p, :], ALU.add).then_inc(S["z_ok"], 1)
                if do_cross:
                    after(dve, "ot_mm", n)
                    o = b6[:, :].rearrange("p (g k e) -> p g k e", g=XG, k=XKV)
                    dve.reciprocal(rl2[:, :, :], o[:, :, :, XD]).then_inc(S["rl2_ok"], 1)
                    after(dve, "rl2_ok", n)
                    dve.tensor_tensor(a2[:, :].rearrange("p (g k d) -> p g k d", g=XG, k=XKV), o[:, :, :, 0:XD],
                                      rl2[:, :, :].unsqueeze(3).to_broadcast([P, XG, XKV, XD]), ALU.mult).then_inc(S["a2_ok"], 1)
                    after(dve, "a2_ok", n)
                    dve.tensor_tensor(res2[:, :], a2[:, :], x1[:, q, :], ALU.add).then_inc(S["res2_ok"], 1)
                    after(dve, "res2_ok", n)
                    norm(n - 1, res2[:, :], st2[:, :], mv2[:, :], va2[:, :], 2)
                    after(dve, "rs2_ok", n)
                    dve.tensor_scalar(x2[:, q, :], res2[:, :], mv2[:, 0:1], rs2[:, 0:1],
                                      ALU.subtract, ALU.mult).then_inc(S["x2_ok"], 1)

            steps(dve, step)

            done = [0]

            def link(instruction):
                done[0] += 1
                instruction.then_inc(S["route"], 1)
                dve.wait_ge(S["route"], done[0])

            after(dve, "rank_mm", 1)
            link(dve.tensor_copy(tot[:, :, :].rearrange("p t e -> p (t e)"), b6[:, 64:128]))
            link(dve.memset(base[:, 0, :], 0.0))
            for t in range(1, TILES):
                link(dve.tensor_tensor(base[:, t, :], base[:, t - 1, :], tot[:, t - 1, :], ALU.add))
            link(dve.tensor_tensor(cnt[:, :], base[:, TILES - 1, :], tot[:, TILES - 1, :], ALU.add))
            link(dve.tensor_tensor(over[:, :, :], cnt[:, :].unsqueeze(2).to_broadcast([P, NE, 8]),
                                   cst[:, C_STEP:C_STEP + 8].unsqueeze(1).to_broadcast([P, NE, 8]), ALU.is_gt))
            link(dve.tensor_reduce(nb[:, :], over[:, :, :], AX, ALU.add))
            link(dve.tensor_tensor(bef[:, :, :], nb[:, :].unsqueeze(1).to_broadcast([P, NE, NE]),
                                   cst[:, C_BEFORE:C_BEFORE + NE * NE].rearrange("p (a b) -> p a b", a=NE), ALU.mult))
            link(dve.tensor_reduce(bst[:, :], bef[:, :, :], AX, ALU.add))
            link(dve.tensor_scalar(bst128[:, :], bst[:, :], float(P), None, ALU.mult))
            link(dve.tensor_tensor(slot1[:, :, :], base[:, :, :],
                                   bst128[:, :].unsqueeze(1).to_broadcast([P, TILES, NE]), ALU.add))
            link(dve.tensor_tensor(slot2[:, :, :], b6[:, 0:64].rearrange("p (t e) -> p t e", t=TILES),
                                   slot1[:, :, :], ALU.add))
            link(dve.tensor_tensor(slot3[:, :, :], slot2[:, :, :], onehot[:, :, :], ALU.mult))
            link(dve.tensor_reduce(posf[:, :], slot3[:, :, :], AX, ALU.add))
            dve.tensor_copy(pos[:, :], posf[:, :]).then_inc(S["pos_ok"], 1)
            link(dve.tensor_tensor(bend[:, :], bst[:, :], nb[:, :], ALU.add))
            link(dve.tensor_tensor(ebc[:, :, :], bend[:, :].unsqueeze(1).to_broadcast([P, BLOCKS, NE]),
                                   cst[:, C_BLOCK:C_BLOCK + BLOCKS].unsqueeze(2).to_broadcast([P, BLOCKS, NE]), ALU.is_le))
            link(dve.tensor_reduce(ebf[:, :], ebc[:, :, :], AX, ALU.add))
            link(dve.tensor_scalar(ebm[:, :], ebf[:, :], float(NE - 1), None, ALU.min))
            dve.tensor_copy(ebi[:, :], ebm[:, :]).then_inc(S["ebi_ok"], 1)

            def hidden(j, p):
                g = sA[:, 512 * p:512 * p + F]
                u = sA[:, 512 * p + F:512 * p + 2 * F]
                after(dve, "eg_ok", j + 1)
                dve.tensor_scalar(ed[:, p, :], eg[:, p, :], 1.0, None, ALU.add).then_inc(S["ed_ok"], 1)
                after(dve, "ed_ok", j + 1)
                dve.reciprocal(er[:, p, :], ed[:, p, :]).then_inc(S["er_ok"], 1)
                after(dve, "er_ok", j + 1)
                dve.tensor_tensor(eh[:, p, :], g, er[:, p, :], ALU.mult).then_inc(S["eh_ok"], 1)
                after(dve, "eh_ok", j + 1)
                after(dve, "ehT_mm", j - 1)
                dve.tensor_tensor(ehid[:, p, :], u, eh[:, p, :], ALU.mult).then_inc(S["ehid_ok"], 1)

            def dve_blocks(it):
                for u in range(2):
                    hidden(2 * it + 1 + u, 1 - u)

            hidden(0, 0)
            expert_turns(dve, dve_blocks)

            def finish(t):
                after(dve, "rs3_ok", t + 1)
                dve.tensor_scalar(fin[:, t, :], res3[:, t, :], mv3[:, t, 0:1], rs3[:, t:t + 1],
                                  ALU.subtract, ALU.mult).then_inc(S["fin_ok"], 1)

            for t in range(TILES):
                dve.wait_ge(d_yg[t], 16)
                dve.tensor_tensor(res3[:, t, :], yg[:, t, :], z_all[:, t, :], ALU.add).then_inc(S["res3_ok"], 1)
                after(dve, "res3_ok", t + 1)
                norm(t, res3[:, t, :], st3[:, t, :], mv3[:, t, :], va3[:, t:t + 1], 3)
                if t >= 1:
                    finish(t - 1)
            finish(TILES - 1)


def channel_order():
    import numpy as np

    return np.arange(E).reshape(XKV, XG, XD).transpose(1, 0, 2).reshape(-1)


def natural_order(y):
    import numpy as np

    out = np.empty_like(y)
    out[..., channel_order()] = y
    return out


def decoder_layout(i):
    import numpy as np

    def rows(w):
        return w.reshape(-1, P, w.shape[1]).transpose(1, 0, 2)

    a = {k: np.asarray(v) for k, v in i.items()}
    x = a["x"].reshape(TILES, P, E)
    order = channel_order()
    ctx = a["ctx_512"]
    ffn = [np.concatenate([rows(np.concatenate([g, u], 1)[order]).reshape(P, -1), rows(d[:, order]).reshape(P, -1)], 1) for g, u, d in
           [(a["L0_ffn_gate_w"][e], a["L0_ffn_up_w"][e], a["L0_ffn_down_w"][e]) for e in range(NE)]
           + [(a["L0_ffn_shared_gate_w"], a["L0_ffn_shared_up_w"], a["L0_ffn_shared_down_w"])]]
    small = np.stack([
        a["L0_attn_w_k_down"], a["L0_attn_w_v_down"],
        a["L0_attn_q_to_latent"].transpose(2, 0, 1).reshape(L, E),
        a["L0_attn_v_up"].reshape(H // 2, 2, L, D).transpose(2, 1, 0, 3).reshape(L, E)], 1)
    c = np.zeros((P, C_WIDTH), np.float32)
    c[:, C_IDENT:C_IDENT + P] = np.eye(P)
    c[:, C_EXPERT:C_EXPERT + NE] = np.arange(NE)
    c[:, C_STEP:C_STEP + 8] = P * np.arange(8)
    c[:, C_BEFORE:C_BEFORE + NE * NE] = np.tril(np.ones((NE, NE)), -1).reshape(-1)
    c[:, C_BLOCK:C_BLOCK + BLOCKS] = np.arange(BLOCKS)
    c[:, C_POW] = -0.5
    m = np.zeros((P, M_WIDTH), np.float32)
    m[:, M_IDENT:M_IDENT + P] = np.eye(P)
    t = np.arange(P) % T
    m[:, M_CAUSAL:M_CAUSAL + 512] = np.where(np.arange(512)[None] % T <= t[:, None], 0.0, -1e30)
    m[:, M_RANK:M_RANK + P] = np.triu(np.ones((P, P)), 1)
    m[:, M_ONES:M_ONES + P] = 1.0
    return {
        "x": x[:, :, order],
        "xT": x.reshape(TILES, P, KC, P).transpose(0, 3, 2, 1),
        "ctx_k": ctx.reshape(TILES, 2, T, XKV, XD).transpose(1, 3, 4, 0, 2),
        "ctx_v": ctx,
        "w_q": rows(a["L0_attn_w_q"].T),
        "w_small": small,
        "w_out": rows(a["L0_attn_w_out"].T[:, order]),
        "w_ffn": np.stack(ffn),
        "router": rows(a["L0_ffn_router_w"][order]),
        "consts": c,
        "masks": m,
    }


def build_program(nc, shapes):
    args = [nc.dram_tensor(name, shape, dt, kind="ExternalInput").ap() for name, shape, dt in shapes]
    out = nc.dram_tensor("out", (TILES, P, E), F32, kind="ExternalOutput").ap()
    decoder_layer(nc, *args, out)


def kernel(**inputs):
    import numpy as np
    import concourse.bacc as bacc
    from concourse.bass_utils import run_bass_kernel_spmd

    nc = bacc.Bacc("TRN2", target_bir_lowering=False, num_devices=1)
    arrays = {k: np.ascontiguousarray(v) for k, v in decoder_layout(inputs).items()}
    build_program(nc, [(k, v.shape, mybir.dt.from_np(v.dtype)) for k, v in arrays.items()])
    r = run_bass_kernel_spmd(nc, [arrays], core_ids=[0])
    return natural_order(r.results[0]["out"].reshape(B, T, E))
```

```python
from contextlib import ExitStack

import concourse.bass as bass
from concourse import mybir

F32 = mybir.dt.float32
BF16 = mybir.dt.bfloat16
U32 = mybir.dt.uint32
I32 = mybir.dt.int32
ALU = mybir.AluOpType
ACT = mybir.ActivationFunctionType
AX = mybir.AxisListType.X

P = 128
B, T, E = 16, 64, 256
TILES = B * T // P
H, D = 16, 16
L = 64
KC = E // P
HG = P // D
XKV, XG, XD = 8, 4, 8
CX = XKV * XD
NE = 8
F = 256
WROW = KC * 2 * F + KC * E
BLOCKS = (B * T - NE) // P + NE
SLOTS = BLOCKS * P
SELF_SCALE = 1.5 / float(L) ** 0.5
CROSS_SCALE = 1.0 / float(XD) ** 0.5
EPS = 1e-5

C_IDENT, C_EXPERT, C_STEP, C_BEFORE, C_BLOCK, C_EPS, C_POW = 0, 128, 136, 144, 208, 223, 224
C_WIDTH = 225
M_IDENT, M_CAUSAL, M_RANK, M_ONES = 0, 128, 640, 768
M_WIDTH = 896


def decoder_layer(nc, x, xT, ctx_k, ctx_v, w_q, w_small, w_out, w_ffn, router, consts, masks, out):
    with ExitStack() as stack:
        def sb(name, shape, dt=F32):
            return stack.enter_context(nc.sbuf_tensor(name, shape, dt))

        def bank(name, n=1):
            return stack.enter_context(nc.psum_tensor(name, [P, 512 * n], F32))

        def sem(name):
            return stack.enter_context(nc.semaphore(name))

        cst = sb("cst", [P, C_WIDTH])
        msk = sb("msk", [P, M_WIDTH], BF16)
        wq = sb("wq", [P, KC, E])
        wsm = sb("wsm", [L, 4, E])
        wk = sb("wk", [P, KC, E])
        wv = sb("wv", [P, KC, 2, P])
        wo = sb("wo", [P, KC, E])
        wrt = sb("wrt", [P, KC, NE])
        wff = sb("wff", [P, NE + 1, WROW])
        x_all = sb("x_all", [P, TILES, E])
        x2T_all = x_all
        z_all = sb("z_all", [P, TILES, E])
        kx = sb("kx", [P, TILES, 2, 512])
        vnat = sb("vnat", [P, B, CX])
        onehot = sb("onehot", [P, TILES, NE], BF16)
        xTt = sb("xTt", [P, 2, KC, P])
        qT = sb("qT", [P, 2, 2, P])
        kT = sb("kT", [P, 2, 2, 2, T])
        kbd = sb("kbd", [P, 2, 2, 2, 512])
        vbd = sb("vbd", [P, 2, 2, 8, 32])
        m1 = sb("m1", [P, H])
        p1 = sb("p1", [P, H, T])
        msk32 = p1[:, :, :].rearrange("p h s -> p (h s)")[:, 0:M_WIDTH]
        l1 = sb("l1", [P, H])
        r1 = sb("r1", [P, H])
        p1n = sb("p1n", [P, H, T])
        p1T = sb("p1T", [P, 8, P])
        cT = sb("cT", [P, 2, P])
        res1 = sb("res1", [P, E])
        st1 = sb("st1", [P, 6])
        mv1 = sb("mv1", [P, 2])
        va1 = sb("va1", [P, 1])
        rs1 = sb("rs1", [P, 1])
        x1 = sb("x1", [P, 2, E])
        qx = sb("qx", [P, XG, T])
        m2 = sb("m2", [P, 2, 2 * XKV])
        p2 = sb("p2", [P, 2, 2 * XKV, T])
        p2T = sb("p2T", [P, 2, 4, 2, P])
        vx = sb("vx", [P, 2, 2, 4, 2, 16])
        oT = sb("oT", [P, XG, 2, T])
        rl2 = sb("rl2", [P, XG, XKV])
        a2 = sb("a2", [P, E])
        res2 = sb("res2", [P, E])
        st2 = sb("st2", [P, 6])
        mv2 = sb("mv2", [P, 2])
        va2 = sb("va2", [P, 1])
        rs2 = sb("rs2", [P, 1])
        x2 = sb("x2", [P, 2, E])
        x2s = sb("x2s", [P, KC, P])
        top = sb("top", [P, 8])
        topi = sb("topi", [P, 8], U32)
        topf = sb("topf", [P, 1])
        sc_t = sb("sc_t", [P, 1])
        score = sb("score", [P, 1])
        xs = sb("xs", [P, TILES, E])
        tot = sb("tot", [P, TILES, NE])
        base = sb("base", [P, TILES, NE])
        cnt = sb("cnt", [P, NE])
        over = sb("over", [P, NE, 8])
        nb = sb("nb", [P, NE])
        bef = sb("bef", [P, NE, NE])
        bst = sb("bst", [P, NE])
        bend = sb("bend", [P, NE])
        bst128 = sb("bst128", [P, NE])
        slot1 = sb("slot1", [P, TILES, NE])
        slot2 = sb("slot2", [P, TILES, NE])
        slot3 = sb("slot3", [P, TILES, NE])
        posf = sb("posf", [P, TILES])
        pos = sb("pos", [P, TILES], U32)
        ebc = sb("ebc", [P, BLOCKS, NE])
        ebf = sb("ebf", [P, BLOCKS])
        ebm = sb("ebm", [P, BLOCKS])
        ebi = sb("ebi", [P, BLOCKS], I32)
        room = kx[:, :, :, :].rearrange("p t s n -> p (t s n)")
        xe, th, gt, hid, ye = (room[:, 2 * E * i:2 * E * i + 2 * E].rearrange("p (a n) -> p a n", a=2)
                               for i in range(5))
        xeT, hT = (room[:, 2 * E * i:2 * E * i + 2 * E].rearrange("p (a k n) -> p a k n", a=2, k=KC)
                   for i in range(5, 7))
        zero = sb("zero", [P, E])
        yg, res3 = xs, z_all
        st3 = sb("st3", [P, TILES, 6])
        mv3 = sb("mv3", [P, TILES, 2])
        va3 = sb("va3", [P, TILES])
        rs3 = sb("rs3", [P, TILES])
        fin = x_all

        xs_sorted = nc.dram_tensor("xs_sorted", (SLOTS, E), F32, kind="Internal").ap()
        ys_sorted = nc.dram_tensor("ys_sorted", (SLOTS, E), F32, kind="Internal").ap()

        def sorted_rows(rows, j):
            return rows.rearrange("(j p) c -> j p c", p=P)[j]

        sA = bank("sA", 2)
        sB = bank("sB", 2)
        tp = [bank("tp0"), bank("tp1")]
        b6 = bank("b6")
        b7 = bank("b7")

        ident = cst[:, C_IDENT:C_IDENT + P]

        def flat(ap):
            names = "abcdef"[:len(ap.shape) - 1]
            return ap.rearrange(f"p {' '.join(names)} -> p ({' '.join(names)})")

        d_wq, d_msk, d_cst, d_wo, d_wrt, d_small, d_x, d_kx, d_vn, d_ffn, d_shared = (sem(s) for s in (
            "d_wq", "d_msk", "d_cst", "d_wo", "d_wrt", "d_small", "d_x", "d_kx", "d_vn", "d_ffn", "d_shared"))
        d_zero = sem("d_zero")
        d_xT = [sem("d_xT0"), sem("d_xT1")]
        d_kbd = [sem("d_kbd0"), sem("d_kbd1")]
        d_disp = sem("d_disp")
        passed = sem("passed")
        d_xe = [sem(f"d_xe{i}") for i in range(2)]
        d_ye = [sem(f"d_ye{i}") for i in range(2)]
        d_yg = [sem(f"d_yg{i}") for i in range(TILES)]
        d_out = sem("d_out")
        kbd_zeroed, vbd_zeroed, kx_zeroed, vx_zeroed, zero_ok = (sem(s) for s in (
            "kbd_zeroed", "vbd_zeroed", "kx_zeroed", "vx_zeroed", "zero_ok"))
        fuse_mm, fuse_cp, msk_ok = sem("fuse_mm"), sem("fuse_cp"), sem("msk_ok")
        names = """qk_mm v_mm q_cp k_cp v_cp s1_mm m1_ok sub1 exp1 sum1 rec1 nrm1
        pt1a_mm pt1b_mm pt1a_cp pt1b_cp c_mm c_cp o1_mm res1_ok st1_ok mv1_ok va1_ok rs1_ok x1_ok
        qx_mm qx_cp s2a_mm s2b_mm m2a m2b sub2a sub2b exp2a exp2b pt2_mm0 pt2_mm1 pt2_mm2 pt2_mm3
        pt2_cp0 pt2_cp1 pt2_cp2 pt2_cp3 vx_half vx_ok o2_mm o2_cp ot_mm rl2_ok a2_ok res2_ok st2_ok
        mv2_ok va2_ok rs2_ok x2_ok x2T_mm x2T_cp lg_mm top_ok topi_ok topf_ok hot_ok sct_ok score_ok
        x2_kept x2T_kept xs_ok rank_mm route ebi_ok pos_ok
        xeT_mm xeT_cp gu_mm th_ok gt_ok hid_ok hT_mm hT_cp dn_mm z_ok ye_ok
        res3_ok st3_ok mv3_ok va3_ok rs3_ok fin_ok""".split()
        S = {name: sem(name) for name in names}

        def after(eng, name, count):
            if isinstance(count, int) and count <= 0:
                return
            eng.wait_ge(S[name], count)

        def after_alone(eng, name, count):
            after(eng, name, count)
            eng.sem_inc(passed, 1)

        def steps(eng, step):
            def peeled(n):
                step(n, n // 2, n % 2, n < TILES, 1 <= n <= TILES, n >= 2, n + 1 < TILES)

            peeled(0)
            peeled(1)
            with eng.Fori(1, TILES // 2 - 1) as it:
                for p in range(2):
                    step(2 * it + p, it, p, True, True, True, True)
            for n in range(TILES - 2, TILES + 2):
                peeled(n)

        block = stack.enter_context(nc.Block())

        @block.sync
        def _(sp):
            sp.dma_start(wsm[:, :, :], w_small).then_inc(d_small, 16)
            sp.dma_start(xTt[:, 0, :, :], xT[0]).then_inc(d_xT[0], 16)
            sp.dma_start(wq[:, :, :], w_q).then_inc(d_wq, 16)
            sp.dma_start(msk32, masks).then_inc(d_msk, 16)
            sp.dma_start(cst[:, :], consts).then_inc(d_cst, 16)
            sp.dma_start(xTt[:, 1, :, :], xT[1]).then_inc(d_xT[1], 16)
            sp.dma_start(x_all[:, :, :], x.rearrange("t p c -> p t c")).then_inc(d_x, 16)
            sp.dma_start(wo[:, :, :], w_out).then_inc(d_wo, 16)
            sp.dma_start(wrt[:, :, :], router).then_inc(d_wrt, 16)
            def diagonal(p):
                for h in range(HG):
                    sp.dma_start(kbd[D * h:D * h + D, p, :, :, T * h:T * h + T],
                                 kT[D * h:D * h + D, p, :, :, :]).then_inc(d_kbd[p], 16)

            def load(n, half, p, *_):
                after_alone(sp, "k_cp", n + 1)
                after_alone(sp, "s1_mm", n - 1)
                diagonal(p)

            def load_xT(n, p):
                after_alone(sp, "qk_mm", n + 1)
                sp.dma_start(xTt[:, p, :, :], xT[n + 2]).then_inc(d_xT[p], 16)

            sp.wait_ge(kbd_zeroed, 1)
            load(0, 0, 0)
            load_xT(0, 0)
            sp.wait_ge(kx_zeroed, 1)
            for b in range(2):
                for kv in range(XKV):
                    r = CX * b + XD * kv
                    sp.dma_start(kx[r:r + XD, :, b, T * kv:T * kv + T], ctx_k[b, kv]).then_inc(d_kx, 16)
            load(1, 0, 1)
            load_xT(1, 1)
            for half in range(2):
                sp.dma_start(vnat[64 * half:64 * half + 64, :, :], ctx_v.rearrange("b s c -> s b c")).then_inc(d_vn, 16)
            sp.dma_start(wff[:, NE, :], w_ffn[NE]).then_inc(d_shared, 16)
            with sp.Fori(1, TILES // 2 - 1) as it:
                for p in range(2):
                    load(2 * it + p, it, p)
                    load_xT(2 * it + p, p)
            for n in range(TILES - 2, TILES):
                load(n, n // 2, n % 2)

            sp.wait_ge(d_disp, 16 * TILES)

            def load_block(j, p):
                after_alone(sp, "xeT_mm", j - 1)
                sp.dma_start(xe[:, p, :], sorted_rows(xs_sorted, j)).then_inc(d_xe[p], 16)

            def store_block(j, p):
                after_alone(sp, "ye_ok", j + 1)
                sp.dma_start(sorted_rows(ys_sorted, j), ye[:, p, :]).then_inc(d_ye[p], 16)

            for e in range(4):
                load_block(e, e % 2)
                if e == 3:
                    store_block(0, 0)
            with sp.Fori(2, BLOCKS // 2) as it:
                for p in range(2):
                    load_block(2 * it + p, p)
                    store_block(2 * it + p - 3, 1 - p)
            load_block(BLOCKS - 1, 0)
            for e in range(BLOCKS - 4, BLOCKS):
                store_block(e, e % 2)
            for t in range(TILES):
                after(sp, "fin_ok", t + 1)
                sp.dma_start(out[t], fin[:, t, :]).then_inc(d_out, 16)
            sp.wait_ge(d_out, 16 * TILES)

        @block.gpsimd
        def _(pool):
            pool.memset(kbd[:, :, :, :, :], 0.0).then_inc(kbd_zeroed, 1)
            pool.memset(vx[:, :, :, :, :, :], 0.0).then_inc(vx_zeroed, 1)
            pool.wait_ge(vx_zeroed, 1)
            for kv in range(2):
                pool.memset(vx[64 * kv:64 * kv + 64, :, :, :, kv, XD:XD + 1], 1.0).then_inc(vx_zeroed, 1)
                pool.wait_ge(vx_zeroed, 2 + kv)
            pool.memset(kx[:, :, :, :], 0.0).then_inc(kx_zeroed, 1)
            pool.wait_ge(zero_ok, 1)
            for j in range(BLOCKS):
                pool.dma_start(xs_sorted[P * j:P * j + P, :], zero[:, :]).then_inc(d_zero, 16)
            for e in range(NE):
                pool.dma_start(wff[:, e, :], w_ffn[e]).then_inc(d_ffn, 16)
            pool.wait_ge(vx_zeroed, 3)
            pool.wait_ge(d_cst, 16)

            def step(n, half, p, do_self, do_cross, do_ffn, do_proj):
                q = 1 - p
                if do_cross:
                    if isinstance(n, int) and n == 1:
                        pool.wait_ge(d_vn, 32)
                    for kv in range(2):
                        rows = slice(64 * kv, 64 * kv + 64)
                        src = vnat[rows, bass.ds(2 * (n - 1), 2), :].rearrange("p b (k v d) -> p b k v d", k=4, v=2)
                        name = ("vx_half", "vx_ok")[kv]
                        pool.tensor_copy(vx[rows, q, :, :, kv, 0:XD], src[:, :, :, kv, :]).then_inc(S[name], 1)
                        after(pool, name, n)
                if do_self:
                    after(pool, "rec1", n + 1)
                    after(pool, "pt1b_mm", n)
                    pool.tensor_tensor(p1n[:, :, :], p1[:, :, :],
                                       r1[:, :].unsqueeze(2).to_broadcast([P, H, T]), ALU.mult).then_inc(S["nrm1"], 1)
                if do_ffn:
                    after(pool, "x2T_cp", n - 1)
                    pool.tensor_copy(z_all[:, n - 2, :], x2[:, p, :]).then_inc(S["x2_kept"], 1)
                    pool.tensor_copy(x2T_all[:, n - 2, :], flat(x2s[:, :, :])).then_inc(S["x2T_kept"], 1)
                    after(pool, "score_ok", n - 1)
                    pool.tensor_tensor(xs[:, n - 2, :], x2[:, p, :],
                                       score[:, 0:1].to_broadcast([P, E]), ALU.mult).then_inc(S["xs_ok"], 1)
                if do_self:
                    after(pool, "va1_ok", n + 1)
                    pool.tensor_tensor(rs1[:, :], va1[:, :], cst[:, C_POW:C_POW + 1], ALU.pow).then_inc(S["rs1_ok"], 1)
                if do_cross:
                    after(pool, "va2_ok", n)
                    pool.tensor_tensor(rs2[:, :], va2[:, :], cst[:, C_POW:C_POW + 1], ALU.pow).then_inc(S["rs2_ok"], 1)

            steps(pool, step)

            after(pool, "xs_ok", TILES)
            after(pool, "pos_ok", 1)
            pool.wait_ge(d_zero, 16 * BLOCKS)
            for t in range(TILES):
                pool.indirect_dma_start(xs_sorted, bass.IndirectOffsetOnAxis(pos[:, t:t + 1], 0),
                                        xs[:, t, :], None).then_inc(d_disp, 16)
            pool.wait_ge(d_ye[0], 16 * ((BLOCKS + 1) // 2))
            pool.wait_ge(d_ye[1], 16 * (BLOCKS // 2))
            for t in range(TILES):
                pool.indirect_dma_start(yg[:, t, :], None, ys_sorted,
                                        bass.IndirectOffsetOnAxis(pos[:, t:t + 1], 0)).then_inc(d_yg[t], 16)
            for t in range(TILES):
                after(pool, "va3_ok", t + 1)
                pool.tensor_tensor(rs3[:, t:t + 1], va3[:, t:t + 1], cst[:, C_POW:C_POW + 1], ALU.pow).then_inc(S["rs3_ok"], 1)

        @block.tensor
        def _(pe):
            def mm(o, lhsT, rhs, start=True, stop=True, **k):
                return pe.matmul(o, lhsT, rhs, start=start, stop=stop, **k)

            pe.wait_ge(d_small, 16)
            for w in range(2):
                for k in range(KC):
                    last = mm(sB[:, 512 * w + E * k:512 * w + E * k + E], wsm[:, w, P * k:P * k + P], wsm[:, 2 + w, :])
            last.then_inc(fuse_mm, 1)
            pe.wait_ge(fuse_cp, 2)
            pe.wait_ge(d_wq, 16)

            def values(t, half, p):
                pe.wait_ge(d_xT[p], 16 * half + 16)
                for par in range(2):
                    for s in range(2):
                        for k in range(KC):
                            last = mm(tp[1][64 * par:64 * par + 64, P * s:P * s + P], xTt[:, p, k, T * s:T * s + T],
                                      wv[:, k, par, :], start=(k == 0), stop=(k == KC - 1))
                last.then_inc(S["v_mm"], 1)

            def queries_keys(t, p):
                for w, weight in enumerate((wq, wk)):
                    for g in range(2):
                        for k in range(KC):
                            last = mm(tp[0][:, P * (2 * w + g):P * (2 * w + g) + P], weight[:, k, P * g:P * g + P],
                                      xTt[:, p, k, :], start=(k == 0), stop=(k == KC - 1))
                last.then_inc(S["qk_mm"], 1)

            values(0, 0, 0)
            queries_keys(0, 0)
            pe.wait_ge(d_cst, 16)
            pe.wait_ge(msk_ok, 1)
            pe.wait_ge(d_wo, 16)
            pe.wait_ge(d_wrt, 16)

            def step(n, half, p, do_self, do_cross, do_ffn, do_proj):
                q = 1 - p
                if do_self:
                    after(pe, "q_cp", n + 1)
                    pe.wait_ge(d_kbd[p], 16 * HG * (half + 1))
                    after(pe, "sub2b", n - 1)
                    for g in range(2):
                        for s in range(2):
                            o = sA[T * s:T * s + T, 512 * g:512 * g + 512]
                            mm(o, msk[:, M_IDENT + T * s:M_IDENT + T * s + T], msk[:, M_CAUSAL:M_CAUSAL + 512], stop=False)
                            last = mm(o, qT[:, p, g, T * s:T * s + T], kbd[:, p, g, s, :], start=False)
                    last.then_inc(S["s1_mm"], 1)
                if do_cross:
                    after(pe, "x1_ok", n)
                    after(pe, "a2_ok", n - 1)
                    x1v = x1[:, q, :].rearrange("p (g c) -> p g c", g=XG)
                    for s in range(2):
                        for g in range(XG):
                            last = mm(b6[64 * s:64 * s + 64, T * g:T * g + T], x1v[:, g, :],
                                      cst[:, C_IDENT + T * s:C_IDENT + T * s + T])
                    last.then_inc(S["qx_mm"], 1)
                if do_proj:
                    after(pe, "v_cp", n + 1)
                    after(pe, "pt2_cp3", n - 1)
                    values(n + 1, half + p, q)
                if do_cross:
                    after(pe, "qx_cp", n)
                    after(pe, "sub2a", n - 1)
                    if isinstance(n, int) and n == 1:
                        pe.wait_ge(d_kx, 16 * 2 * XKV)
                    for s in range(2):
                        last = mm(sB[:, 512 * s:512 * s + 512], flat(qx[:, 0:2, :]), kx[:, n - 1, s, :])
                    last.then_inc(S["s2a_mm"], 1)
                if do_proj:
                    after(pe, "pt2_cp2", n - 1)
                    queries_keys(n + 1, q)
                if do_ffn:
                    after(pe, "x2_ok", n - 1)
                    after(pe, "o2_cp", n - 1)
                    for k in range(KC):
                        last = pe.transpose(b7[:, P * k:P * k + P], x2[:, p, P * k:P * k + P], ident)
                    last.then_inc(S["x2T_mm"], 1)
                    after(pe, "x2T_cp", n - 1)
                    for k in range(KC):
                        last = mm(b7[:, 256:256 + NE], x2s[:, k, :], wrt[:, k, :], start=(k == 0), stop=(k == KC - 1))
                    last.then_inc(S["lg_mm"], 1)
                if do_cross:
                    if do_self:
                        after(pe, "sub1", n + 1)
                    else:
                        after(pe, "sub2b", n - 1)
                    for s in range(2):
                        last = mm(sA[:, 512 * s:512 * s + 512], flat(qx[:, 2:4, :]), kx[:, n - 1, s, :])
                    last.then_inc(S["s2b_mm"], 1)
                if do_self:
                    after(pe, "nrm1", n + 1)
                    for c, bank_ in enumerate(tp):
                        if do_proj:
                            after(pe, ("q_cp", "v_cp")[c], n + 2)
                        else:
                            after(pe, ("pt2_cp2", "pt2_cp3")[c], n - 1)
                        for i in range(4):
                            hp = 4 * c + i
                            last = pe.transpose(bank_[:, P * i:P * i + P], flat(p1n[:, 2 * hp:2 * hp + 2, :]), ident)
                        last.then_inc(S[("pt1a_mm", "pt1b_mm")[c]], 1)
                if do_self:
                    after(pe, "pt1b_cp", n + 1)
                    after(pe, "v_cp", n + 1)
                    if do_ffn:
                        after(pe, "topi_ok", n - 1)
                    for s in range(2):
                        for hp in range(8):
                            r = 32 * (hp % 4)
                            last = mm(b7[r:r + 32, P * (hp // 4) + T * s:P * (hp // 4) + T * s + T],
                                      vbd[:, p, s, hp, :], p1T[:, hp, T * s:T * s + T])
                    last.then_inc(S["c_mm"], 1)
                def probs(gp):
                    after(pe, ("exp2a", "exp2b")[gp], n)
                    for s in range(2):
                        if gp == 1:
                            after(pe, f"pt2_cp{s}", n)
                        elif do_self:
                            after(pe, ("pt1a_cp", "pt1b_cp")[s], n + 1)
                        else:
                            after(pe, f"pt2_cp{2 + s}", n - 1)
                        for i in range(4):
                            last = pe.transpose(tp[s][:, P * i:P * i + P],
                                                flat(p2[:, gp, XKV * s + 2 * i:XKV * s + 2 * i + 2, :]), ident)
                        last.then_inc(S[f"pt2_mm{2 * gp + s}"], 1)

                if do_cross:
                    probs(0)
                if do_self:
                    after(pe, "c_cp", n + 1)
                    for g in range(KC):
                        last = mm(b7[:, 0:E], cT[:, g, :], wo[:, g, :], start=(g == 0), stop=(g == KC - 1))
                    last.then_inc(S["o1_mm"], 1)
                if do_cross:
                    probs(1)
                if do_cross:
                    after(pe, "pt2_cp3", n)
                    after(pe, "vx_ok", n)
                    if do_self:
                        after(pe, "res1_ok", n + 1)
                    else:
                        after(pe, "topi_ok", n - 1)
                    for s in range(2):
                        for kp in range(4):
                            last = mm(b7[32 * kp:32 * kp + 32, 256 * s:256 * s + 256], flat(vx[:, q, s, kp, :, :]),
                                      flat(p2T[:, s, kp, :, :]))
                    last.then_inc(S["o2_mm"], 1)
                    after(pe, "o2_cp", n)
                    for g in range(XG):
                        last = pe.transpose(b6[:, P * g:P * g + P], flat(oT[:, g, :, :]), ident)
                    last.then_inc(S["ot_mm"], 1)

            steps(pe, step)

            after(pe, "hot_ok", TILES)
            after(pe, "a2_ok", TILES)
            hot = onehot[:, :, :].rearrange("p t e -> p (t e)")
            mm(b6[:, 0:TILES * NE], msk[:, M_RANK:M_RANK + P], hot)
            mm(b6[:, 64:64 + TILES * NE], msk[:, M_ONES:M_ONES + P], hot, skip_group_check=True).then_inc(S["rank_mm"], 1)

            def rows_of(e, p, half):
                pe.wait_ge(d_xe[p], 16 * (half + 1))
                for k in range(KC):
                    last = pe.transpose(tp[p][:, P * k:P * k + P], xe[:, p, P * k:P * k + P], ident)
                last.then_inc(S["xeT_mm"], 1)

            def up(j, p, rows, weights):
                for k in range(KC):
                    last = mm(sA[:, 512 * p:512 * p + 512], rows(k), weights(2 * F * k, 2 * F),
                              start=(k == 0), stop=(k == KC - 1))
                last.then_inc(S["gu_mm"], 1)

            def transpose_hidden(j, p):
                after(pe, "hid_ok", j + 1)
                for k in range(KC):
                    last = pe.transpose(sB[:, 512 * p + P * k:512 * p + P * k + P], hid[:, p, P * k:P * k + P], ident)
                last.then_inc(S["hT_mm"], 1)

            def down(j, p, weights):
                after(pe, "hT_cp", j + 1)
                for k in range(KC):
                    last = mm(sB[:, 512 * p + E:512 * p + 2 * E], hT[:, p, k, :], weights(KC * 2 * F + E * k, E),
                              start=(k == 0), stop=(k == KC - 1))
                last.then_inc(S["dn_mm"], 1)

            def shared(c, n):
                return wff[:, NE, c:c + n]

            def expert_of(e):
                chosen = pe.value_load(ebi[0:1, bass.ds(e, 1)], min_val=0, max_val=NE - 1)
                return lambda c, n: flat(wff[:, bass.ds(chosen, 1), c:c + n])

            pe.wait_ge(d_shared, 16)

            def shared_turn(j):
                p = j % 2
                if j >= 2:
                    after(pe, "z_ok", j - 3)
                    transpose_hidden(j - 2, p)
                    down(j - 2, p, shared)
                after(pe, "x2T_kept", j + 1)
                up(j, p, lambda k: x2T_all[:, j, P * k:P * k + P], shared)

            for j in range(TILES):
                shared_turn(j)

            pe.wait_ge(d_ffn, 16 * NE)
            after(pe, "ebi_ok", 1)

            def expert_turn(e, p, half):
                if isinstance(e, int) and e < 4:
                    after(pe, "z_ok", TILES + e - 3)
                else:
                    after(pe, "ye_ok", e - 3)
                transpose_hidden(TILES + e - 2, p)
                rows_of(e, p, half)
                if isinstance(e, int) and e < 2:
                    weights_down = shared
                else:
                    weights_down = expert_of(e - 2)
                weights_up = expert_of(e)
                down(TILES + e - 2, p, weights_down)
                after(pe, "xeT_cp", e + 1)
                up(TILES + e, p, lambda k: xeT[:, p, k, :], weights_up)

            for e in range(4):
                expert_turn(e, e % 2, e // 2)
            with pe.Fori(2, BLOCKS // 2) as it:
                for p in range(2):
                    expert_turn(2 * it + p, p, it)
            expert_turn(BLOCKS - 1, 0, BLOCKS // 2)
            for e in range(BLOCKS - 2, BLOCKS):
                after(pe, "ye_ok", e - 1)
                transpose_hidden(TILES + e, e % 2)
                down(TILES + e, e % 2, expert_of(e))

        @block.scalar
        def _(act):
            act.wait_ge(fuse_mm, 1)
            act.copy(flat(wk[:, :, :]), sB[:, 0:512]).then_inc(fuse_cp, 1)

            def copy_qk(t, p):
                after(act, "qk_mm", t + 1)
                act.copy(flat(kT[:, p, :, :, :]), tp[0][:, E:2 * E]).then_inc(S["k_cp"], 1)
                act.mul(flat(qT[:, p, :, :]), tp[0][:, 0:E], SELF_SCALE).then_inc(S["q_cp"], 1)

            copy_qk(0, 0)
            act.wait_ge(d_msk, 16)
            act.copy(msk[:, :], msk32).then_inc(msk_ok, 1)

            def step(n, half, p, do_self, do_cross, do_ffn, do_proj):
                q = 1 - p
                if do_cross:
                    after(act, "qx_mm", n)
                    act.mul(flat(qx[:, :, :]), b6[:, 0:E], CROSS_SCALE).then_inc(S["qx_cp"], 1)
                if do_self:
                    after(act, "sub1", n + 1)
                    act.activation(p1[:, :, :], p1[:, :, :], ACT.Exp).then_inc(S["exp1"], 1)
                if do_proj:
                    copy_qk(n + 1, q)
                if do_ffn:
                    after(act, "x2T_mm", n - 1)
                    act.copy(flat(x2s[:, :, :]), b7[:, 0:E]).then_inc(S["x2T_cp"], 1)
                if do_cross:
                    after(act, "sub2a", n)
                    act.activation(p2[:, 0, :, :], p2[:, 0, :, :], ACT.Exp).then_inc(S["exp2a"], 1)
                if do_ffn:
                    after(act, "top_ok", n - 1)
                    act.activation(sc_t[:, :], top[:, 0:1], ACT.Tanh, scale=0.5).then_inc(S["sct_ok"], 1)
                if do_self:
                    after(act, "pt1a_mm", n + 1)
                    after(act, "c_mm", n)
                    act.copy(flat(p1T[:, 0:4, :]), tp[0][:, :]).then_inc(S["pt1a_cp"], 1)
                    after(act, "pt1b_mm", n + 1)
                    act.copy(flat(p1T[:, 4:8, :]), tp[1][:, :]).then_inc(S["pt1b_cp"], 1)
                if do_self:
                    after(act, "c_mm", n + 1)
                    act.copy(flat(cT[:, :, :]), b7[:, 0:E]).then_inc(S["c_cp"], 1)
                if do_cross:
                    after(act, "o2_mm", n - 1)
                    for gp in range(2):
                        if gp == 1:
                            after(act, "sub2b", n)
                            act.activation(p2[:, 1, :, :], p2[:, 1, :, :], ACT.Exp).then_inc(S["exp2b"], 1)
                        for s in range(2):
                            after(act, f"pt2_mm{2 * gp + s}", n)
                            act.copy(p2T[:, s, :, gp, :], tp[s][:, :].rearrange("p (k t) -> p k t", k=4)).then_inc(
                                S[f"pt2_cp{2 * gp + s}"], 1)
                if do_cross:
                    after(act, "o2_mm", n)
                    act.copy(oT[:, :, :, :], b7[:, :].rearrange("p (s g t) -> p g s t", s=2, g=XG)).then_inc(S["o2_cp"], 1)

            steps(act, step)

            def copy_rows(e, p):
                after(act, "xeT_mm", e + 1)
                after(act, "gu_mm", TILES + e - 1)
                act.copy(flat(xeT[:, p, :, :]), tp[p][:, 0:E]).then_inc(S["xeT_cp"], 1)

            def tanh_gate(j, p):
                after(act, "gu_mm", j + 1)
                after(act, "gt_ok", j - 1)
                act.activation(th[:, p, :], sA[:, 512 * p:512 * p + F], ACT.Tanh, scale=0.5).then_inc(S["th_ok"], 1)

            def copy_hidden(j, p):
                after(act, "hT_mm", j + 1)
                after(act, "dn_mm", j - 1)
                act.copy(flat(hT[:, p, :, :]), sB[:, 512 * p:512 * p + E]).then_inc(S["hT_cp"], 1)

            def copy_result(e, p, stored):
                after(act, "dn_mm", TILES + e + 1)
                if not isinstance(stored, int) or stored > 0:
                    act.wait_ge(d_ye[p], 16 * stored)
                act.copy(ye[:, p, :], sB[:, 512 * p + E:512 * p + 2 * E]).then_inc(S["ye_ok"], 1)

            for j in range(TILES):
                if j >= 2:
                    copy_hidden(j - 2, j % 2)
                tanh_gate(j, j % 2)

            def expert_turn(e, p, stored):
                copy_hidden(TILES + e - 2, p)
                copy_rows(e, p)
                if not isinstance(e, int) or e >= 2:
                    copy_result(e - 2, p, stored)
                tanh_gate(TILES + e, p)

            for e in range(4):
                expert_turn(e, e % 2, 0)
            with act.Fori(2, BLOCKS // 2) as it:
                for p in range(2):
                    expert_turn(2 * it + p, p, it - 1)
            expert_turn(BLOCKS - 1, 0, BLOCKS // 2 - 1)
            for e in range(BLOCKS - 2, BLOCKS):
                copy_hidden(TILES + e, e % 2)
                copy_result(e, e % 2, e // 2)

        @block.vector
        def _(dve):
            dve.memset(zero[:, :], 0.0).then_inc(zero_ok, 1)
            dve.memset(vbd[:, :, :, :, :], 0.0).then_inc(vbd_zeroed, 1)
            dve.wait_ge(vbd_zeroed, 1)
            dve.wait_ge(fuse_mm, 1)
            dve.tensor_copy(flat(wv[:, :, :, :]), sB[:, 512:1024]).then_inc(fuse_cp, 1)

            def copy_v(t, p):
                after(dve, "v_mm", t + 1)
                after(dve, "c_mm", t - 1)
                for par in range(2):
                    rows = slice(64 * par, 64 * par + 64)
                    last = dve.tensor_copy(vbd[rows, p, :, :, D * par:D * par + D],
                                    tp[1][rows, 0:E].rearrange("p (s h d) -> p s h d", s=2, h=8))
                last.then_inc(S["v_cp"], 1)

            copy_v(0, 0)
            dve.wait_ge(d_cst, 16)
            dve.wait_ge(d_x, 16)

            def norm(t, src, stats, mv, va, i):
                dve.bn_stats(stats, src).then_inc(S[f"st{i}_ok"], 1)
                after_alone(dve, f"st{i}_ok", t + 1)
                dve.bn_aggr(mv, stats).then_inc(S[f"mv{i}_ok"], 1)
                after(dve, f"mv{i}_ok", t + 1)
                dve.tensor_scalar(va, mv[:, 1:2], EPS, None, ALU.add).then_inc(S[f"va{i}_ok"], 1)

            def step(n, half, p, do_self, do_cross, do_ffn, do_proj):
                q = 1 - p
                if do_self:
                    after(dve, "s1_mm", n + 1)
                    s1 = sA[:, :].rearrange("p (h s) -> p h s", h=H)
                    dve.tensor_reduce(m1[:, :], s1, AX, ALU.max).then_inc(S["m1_ok"], 1)
                    after(dve, "m1_ok", n + 1)
                    after(dve, "nrm1", n)
                    dve.tensor_tensor(p1[:, :, :], s1, m1[:, :].unsqueeze(2).to_broadcast([P, H, T]),
                                      ALU.subtract).then_inc(S["sub1"], 1)
                if do_proj:
                    copy_v(n + 1, q)

                def cross_max(gp, s_, mm_name):
                    after(dve, mm_name, n)
                    s2 = s_[:, :].rearrange("p (k s) -> p k s", k=2 * XKV)
                    name = "ab"[gp]
                    dve.tensor_reduce(m2[:, gp, :], s2, AX, ALU.max).then_inc(S[f"m2{name}"], 1)
                    after(dve, f"m2{name}", n)
                    after(dve, f"pt2_mm{2 * gp + 1}", n - 1)
                    dve.tensor_tensor(p2[:, gp, :, :], s2, m2[:, gp, :].unsqueeze(2).to_broadcast([P, 2 * XKV, T]),
                                      ALU.subtract).then_inc(S[f"sub2{name}"], 1)

                if do_self:
                    after(dve, "exp1", n + 1)
                    dve.tensor_reduce(l1[:, :], p1[:, :, :], AX, ALU.add).then_inc(S["sum1"], 1)
                    after(dve, "sum1", n + 1)
                    dve.reciprocal(r1[:, :], l1[:, :]).then_inc(S["rec1"], 1)
                if do_cross:
                    cross_max(0, sB, "s2a_mm")
                if do_ffn:
                    after_alone(dve, "lg_mm", n - 1)
                    dve.max(top[:, :], b7[:, 256:256 + NE]).then_inc(S["top_ok"], 1)
                    after_alone(dve, "top_ok", n - 1)
                    dve.max_index(topi[:, :], top[:, :], b7[:, 256:256 + NE]).then_inc(S["topi_ok"], 1)
                    after(dve, "topi_ok", n - 1)
                    dve.tensor_copy(topf[:, :], topi[:, 0:1]).then_inc(S["topf_ok"], 1)
                    after(dve, "topf_ok", n - 1)
                    dve.tensor_scalar(onehot[:, n - 2, :], cst[:, C_EXPERT:C_EXPERT + NE], topf[:, 0:1], None,
                                      ALU.is_equal).then_inc(S["hot_ok"], 1)
                if do_cross:
                    cross_max(1, sA, "s2b_mm")
                if do_ffn:
                    after(dve, "sct_ok", n - 1)
                    dve.tensor_scalar(score[:, :], sc_t[:, :], 0.5, 0.5, ALU.mult, ALU.add).then_inc(S["score_ok"], 1)
                if do_self:
                    after(dve, "o1_mm", n + 1)
                    dve.tensor_tensor(res1[:, :], b7[:, 0:E], x_all[:, n, :], ALU.add).then_inc(S["res1_ok"], 1)
                    after(dve, "res1_ok", n + 1)
                    norm(n, res1[:, :], st1[:, :], mv1[:, :], va1[:, :], 1)
                if do_self:
                    after(dve, "rs1_ok", n + 1)
                    after(dve, "res2_ok", n - 1)
                    dve.tensor_scalar(x1[:, p, :], res1[:, :], mv1[:, 0:1], rs1[:, 0:1],
                                      ALU.subtract, ALU.mult).then_inc(S["x1_ok"], 1)
                if do_cross:
                    after(dve, "ot_mm", n)
                    o = b6[:, :].rearrange("p (g k e) -> p g k e", g=XG, k=XKV)
                    dve.reciprocal(rl2[:, :, :], o[:, :, :, XD]).then_inc(S["rl2_ok"], 1)
                    after(dve, "rl2_ok", n)
                    dve.tensor_tensor(a2[:, :].rearrange("p (g k d) -> p g k d", g=XG, k=XKV), o[:, :, :, 0:XD],
                                      rl2[:, :, :].unsqueeze(3).to_broadcast([P, XG, XKV, XD]), ALU.mult).then_inc(S["a2_ok"], 1)
                    after(dve, "a2_ok", n)
                    dve.tensor_tensor(res2[:, :], a2[:, :], x1[:, q, :], ALU.add).then_inc(S["res2_ok"], 1)
                    after(dve, "res2_ok", n)
                    norm(n - 1, res2[:, :], st2[:, :], mv2[:, :], va2[:, :], 2)
                    after(dve, "rs2_ok", n)
                    dve.tensor_scalar(x2[:, q, :], res2[:, :], mv2[:, 0:1], rs2[:, 0:1],
                                      ALU.subtract, ALU.mult).then_inc(S["x2_ok"], 1)

            steps(dve, step)

            done = [0]

            def link(instruction):
                done[0] += 1
                instruction.then_inc(S["route"], 1)
                dve.wait_ge(S["route"], done[0])

            after(dve, "rank_mm", 1)
            link(dve.tensor_copy(tot[:, :, :].rearrange("p t e -> p (t e)"), b6[:, 64:128]))
            link(dve.memset(base[:, 0, :], 0.0))
            for t in range(1, TILES):
                link(dve.tensor_tensor(base[:, t, :], base[:, t - 1, :], tot[:, t - 1, :], ALU.add))
            link(dve.tensor_tensor(cnt[:, :], base[:, TILES - 1, :], tot[:, TILES - 1, :], ALU.add))
            link(dve.tensor_tensor(over[:, :, :], cnt[:, :].unsqueeze(2).to_broadcast([P, NE, 8]),
                                   cst[:, C_STEP:C_STEP + 8].unsqueeze(1).to_broadcast([P, NE, 8]), ALU.is_gt))
            link(dve.tensor_reduce(nb[:, :], over[:, :, :], AX, ALU.add))
            link(dve.tensor_tensor(bef[:, :, :], nb[:, :].unsqueeze(1).to_broadcast([P, NE, NE]),
                                   cst[:, C_BEFORE:C_BEFORE + NE * NE].rearrange("p (a b) -> p a b", a=NE), ALU.mult))
            link(dve.tensor_reduce(bst[:, :], bef[:, :, :], AX, ALU.add))
            link(dve.tensor_scalar(bst128[:, :], bst[:, :], float(P), None, ALU.mult))
            link(dve.tensor_tensor(slot1[:, :, :], base[:, :, :],
                                   bst128[:, :].unsqueeze(1).to_broadcast([P, TILES, NE]), ALU.add))
            link(dve.tensor_tensor(slot2[:, :, :], b6[:, 0:64].rearrange("p (t e) -> p t e", t=TILES),
                                   slot1[:, :, :], ALU.add))
            link(dve.tensor_tensor(slot3[:, :, :], slot2[:, :, :], onehot[:, :, :], ALU.mult))
            link(dve.tensor_reduce(posf[:, :], slot3[:, :, :], AX, ALU.add))
            dve.tensor_copy(pos[:, :], posf[:, :]).then_inc(S["pos_ok"], 1)
            link(dve.tensor_tensor(bend[:, :], bst[:, :], nb[:, :], ALU.add))
            link(dve.tensor_tensor(ebc[:, :, :], bend[:, :].unsqueeze(1).to_broadcast([P, BLOCKS, NE]),
                                   cst[:, C_BLOCK:C_BLOCK + BLOCKS].unsqueeze(2).to_broadcast([P, BLOCKS, NE]), ALU.is_le))
            link(dve.tensor_reduce(ebf[:, :], ebc[:, :, :], AX, ALU.add))
            link(dve.tensor_scalar(ebm[:, :], ebf[:, :], float(NE - 1), None, ALU.min))
            dve.tensor_copy(ebi[:, :], ebm[:, :]).then_inc(S["ebi_ok"], 1)

            def hidden(j, p):
                g = sA[:, 512 * p:512 * p + F]
                u = sA[:, 512 * p + F:512 * p + 2 * F]
                after(dve, "th_ok", j + 1)
                dve.scalar_tensor_tensor(gt[:, p, :], th[:, p, :], 1.0, g, ALU.add, ALU.mult).then_inc(S["gt_ok"], 1)
                after(dve, "gt_ok", j + 1)
                after(dve, "hT_mm", j - 1)
                dve.scalar_tensor_tensor(hid[:, p, :], gt[:, p, :], 0.5, u, ALU.mult, ALU.mult).then_inc(S["hid_ok"], 1)

            def add_shared(t):
                after(dve, "dn_mm", t + 1)
                dve.tensor_tensor(z_all[:, t, :], sB[:, 512 * (t % 2) + E:512 * (t % 2) + 2 * E], z_all[:, t, :], ALU.add).then_inc(S["z_ok"], 1)

            after(dve, "x2_kept", TILES)
            for j in range(TILES):
                if j >= 2:
                    add_shared(j - 2)
                hidden(j, j % 2)
            for e in range(4):
                if e < 2:
                    add_shared(TILES + e - 2)
                hidden(TILES + e, e % 2)
            with dve.Fori(2, BLOCKS // 2) as it:
                for p in range(2):
                    hidden(TILES + 2 * it + p, p)
            hidden(TILES + BLOCKS - 1, 0)

            def finish(t):
                after(dve, "rs3_ok", t + 1)
                dve.tensor_scalar(fin[:, t, :], res3[:, t, :], mv3[:, t, 0:1], rs3[:, t:t + 1],
                                  ALU.subtract, ALU.mult).then_inc(S["fin_ok"], 1)

            for t in range(TILES):
                dve.wait_ge(d_yg[t], 16)
                dve.tensor_tensor(res3[:, t, :], yg[:, t, :], z_all[:, t, :], ALU.add).then_inc(S["res3_ok"], 1)
                after(dve, "res3_ok", t + 1)
                norm(t, res3[:, t, :], st3[:, t, :], mv3[:, t, :], va3[:, t:t + 1], 3)
                if t >= 1:
                    finish(t - 1)
            finish(TILES - 1)


def channel_order():
    import numpy as np

    return np.arange(E).reshape(XKV, XG, XD).transpose(1, 0, 2).reshape(-1)


def natural_order(y):
    import numpy as np

    out = np.empty_like(y)
    out[..., channel_order()] = y
    return out


def decoder_layout(i):
    import numpy as np

    def rows(w):
        return w.reshape(-1, P, w.shape[1]).transpose(1, 0, 2)

    a = {k: np.asarray(v) for k, v in i.items()}
    x = a["x"].reshape(TILES, P, E)
    order = channel_order()
    ctx = a["ctx_512"]
    ffn = [np.concatenate([rows(np.concatenate([g, u], 1)[order]).reshape(P, -1), rows(d[:, order]).reshape(P, -1)], 1) for g, u, d in
           [(a["L0_ffn_gate_w"][e], a["L0_ffn_up_w"][e], a["L0_ffn_down_w"][e]) for e in range(NE)]
           + [(a["L0_ffn_shared_gate_w"], a["L0_ffn_shared_up_w"], a["L0_ffn_shared_down_w"])]]
    small = np.stack([
        a["L0_attn_w_k_down"], a["L0_attn_w_v_down"],
        a["L0_attn_q_to_latent"].transpose(2, 0, 1).reshape(L, E),
        a["L0_attn_v_up"].reshape(H // 2, 2, L, D).transpose(2, 1, 0, 3).reshape(L, E)], 1)
    c = np.zeros((P, C_WIDTH), np.float32)
    c[:, C_IDENT:C_IDENT + P] = np.eye(P)
    c[:, C_EXPERT:C_EXPERT + NE] = np.arange(NE)
    c[:, C_STEP:C_STEP + 8] = P * np.arange(8)
    c[:, C_BEFORE:C_BEFORE + NE * NE] = np.tril(np.ones((NE, NE)), -1).reshape(-1)
    c[:, C_BLOCK:C_BLOCK + BLOCKS] = np.arange(BLOCKS)
    c[:, C_POW] = -0.5
    m = np.zeros((P, M_WIDTH), np.float32)
    m[:, M_IDENT:M_IDENT + P] = np.eye(P)
    t = np.arange(P) % T
    m[:, M_CAUSAL:M_CAUSAL + 512] = np.where(np.arange(512)[None] % T <= t[:, None], 0.0, -1e30)
    m[:, M_RANK:M_RANK + P] = np.triu(np.ones((P, P)), 1)
    m[:, M_ONES:M_ONES + P] = 1.0
    return {
        "x": x[:, :, order],
        "xT": x.reshape(TILES, P, KC, P).transpose(0, 3, 2, 1),
        "ctx_k": ctx.reshape(TILES, 2, T, XKV, XD).transpose(1, 3, 4, 0, 2),
        "ctx_v": ctx,
        "w_q": rows(a["L0_attn_w_q"].T),
        "w_small": small,
        "w_out": rows(a["L0_attn_w_out"].T[:, order]),
        "w_ffn": np.stack(ffn),
        "router": rows(a["L0_ffn_router_w"][order]),
        "consts": c,
        "masks": m,
    }


def build_program(nc, shapes):
    args = [nc.dram_tensor(name, shape, dt, kind="ExternalInput").ap() for name, shape, dt in shapes]
    out = nc.dram_tensor("out", (TILES, P, E), F32, kind="ExternalOutput").ap()
    decoder_layer(nc, *args, out)


def kernel(**inputs):
    import numpy as np
    import concourse.bacc as bacc
    from concourse.bass_utils import run_bass_kernel_spmd

    nc = bacc.Bacc("TRN2", target_bir_lowering=False, num_devices=1)
    arrays = {k: np.ascontiguousarray(v) for k, v in decoder_layout(inputs).items()}
    build_program(nc, [(k, v.shape, mybir.dt.from_np(v.dtype)) for k, v in arrays.items()])
    r = run_bass_kernel_spmd(nc, [arrays], core_ids=[0])
    return natural_order(r.results[0]["out"].reshape(B, T, E))
```

```python
from contextlib import ExitStack

import concourse.bass as bass
from concourse import mybir

F32 = mybir.dt.float32
BF16 = mybir.dt.bfloat16
U32 = mybir.dt.uint32
I32 = mybir.dt.int32
ALU = mybir.AluOpType
ACT = mybir.ActivationFunctionType
AX = mybir.AxisListType.X

P = 128
B, T, E = 16, 64, 256
TILES = B * T // P
H, D = 16, 16
L = 64
KC = E // P
HG = P // D
XKV, XG, XD = 8, 4, 8
CX = XKV * XD
NE = 8
F = 256
WROW = KC * 2 * F + KC * E
BLOCKS = (B * T - NE) // P + NE
SLOTS = BLOCKS * P
SELF_SCALE = 1.5 / float(L) ** 0.5
CROSS_SCALE = 1.0 / float(XD) ** 0.5
EPS = 1e-5
LAST_GROUPS = ((0, 4), (4, 6), (6, TILES))

C_IDENT, C_EXPERT, C_STEP, C_BEFORE, C_BLOCK, C_POW = 0, 128, 136, 144, 208, 224
C_CAUSAL, C_RANK, C_WIDTH = 225, 225 + T, 225 + T + P
M_IDENT, M_CAUSAL, M_RANK, M_ONES, M_WIDTH = 0, 128, 640, 768, 896


def decoder_layer(nc, x, xT, ctx_k, ctx_v, w_q, w_small, w_out, w_ffn, router, consts, out):
    with ExitStack() as stack:
        def sb(name, shape, dt=F32):
            return stack.enter_context(nc.sbuf_tensor(name, shape, dt))

        def bank(name, n=1):
            return stack.enter_context(nc.psum_tensor(name, [P, 512 * n], F32))

        def sem(name):
            return stack.enter_context(nc.semaphore(name))

        cst = sb("cst", [P, C_WIDTH])
        msk = sb("msk", [P, M_WIDTH], BF16)
        wq = sb("wq", [P, KC, E])
        wsm = sb("wsm", [L, 4, E])
        wk = sb("wk", [P, KC, E])
        wv = sb("wv", [P, KC, 2, P])
        wo = sb("wo", [P, KC, E])
        wrt = sb("wrt", [P, KC, NE])
        wff = sb("wff", [P, NE + 1, WROW])
        x_all = sb("x_all", [P, TILES, E])
        x2T_all = x_all
        z_all = sb("z_all", [P, TILES, E])
        kx = sb("kx", [P, TILES, 2, 512])
        vnat = sb("vnat", [P, B, CX])
        onehot = sb("onehot", [P, 2 * TILES + 1, NE], BF16)
        xTt = sb("xTt", [P, 2, KC, P])
        qT = sb("qT", [P, 2, 2, P])
        kT = sb("kT", [P, 2, 2, 2, T])
        kbd = sb("kbd", [P, 2, 2, 2, 512])
        vbd = sb("vbd", [P, 2, 2, 8, 32])
        m1 = sb("m1", [P, H])
        p1 = sb("p1", [P, H, T])
        l1 = sb("l1", [P, H])
        r1 = sb("r1", [P, H])
        p1n = sb("p1n", [P, H, T])
        p1T = sb("p1T", [P, 8, P])
        cT = sb("cT", [P, 2, P])
        res1 = sb("res1", [P, E])
        st1 = sb("st1", [P, 6])
        mv1 = sb("mv1", [P, 2])
        va1 = sb("va1", [P, 1])
        rs1 = sb("rs1", [P, 1])
        x1 = sb("x1", [P, 2, E])
        qx = sb("qx", [P, XG, T])
        m2 = sb("m2", [P, 2, 2 * XKV])
        p2 = sb("p2", [P, 2, 2 * XKV, T])
        p2T = sb("p2T", [P, 2, 4, 2, P])
        vx = sb("vx", [P, 2, 2, 4, 2, 16])
        oT = sb("oT", [P, XG, 2, T])
        rl2 = sb("rl2", [P, XG, XKV])
        a2 = sb("a2", [P, E])
        res2 = sb("res2", [P, E])
        st2 = sb("st2", [P, 6])
        mv2 = sb("mv2", [P, 2])
        va2 = sb("va2", [P, 1])
        rs2 = sb("rs2", [P, 1])
        x2 = sb("x2", [P, 2, E])
        x2s = sb("x2s", [P, KC, P])
        top = sb("top", [P, 8])
        topi = sb("topi", [P, 8], U32)
        topf = sb("topf", [P, 1])
        sc_t = sb("sc_t", [P, 1])
        score = sb("score", [P, 2])
        xs = sb("xs", [P, TILES, E])
        over = sb("over", [P, NE, 8])
        nb = sb("nb", [P, NE])
        bef = sb("bef", [P, NE, NE])
        first = sb("first", [P, NE])
        bend = sb("bend", [P, NE])
        slot = sb("slot", [P, TILES, NE])
        chosen_slot = sb("chosen_slot", [P, TILES, NE])
        posf = sb("posf", [P, TILES])
        pos = sb("pos", [P, TILES], U32)
        ebc = sb("ebc", [P, BLOCKS, NE])
        ebf = sb("ebf", [P, BLOCKS])
        ebm = sb("ebm", [P, BLOCKS])
        ebi = sb("ebi", [P, BLOCKS], I32)
        room = kx[:, :, :, :].rearrange("p t s n -> p (t s n)")
        xe, th, gt, hid, ye = (room[:, 2 * E * i:2 * E * i + 2 * E].rearrange("p (a n) -> p a n", a=2)
                               for i in range(5))
        xeT, hT = (room[:, 2 * E * i:2 * E * i + 2 * E].rearrange("p (a k n) -> p a k n", a=2, k=KC)
                   for i in range(5, 7))
        zero = sb("zero", [P, E])
        yg, res3 = xs, z_all
        st3 = sb("st3", [P, TILES, 6])
        mv3 = sb("mv3", [P, TILES, 2])
        va3 = sb("va3", [P, TILES])
        rs3 = sb("rs3", [P, TILES])
        shift3 = sb("shift3", [P, TILES])
        fin = x_all

        xs_sorted = nc.dram_tensor("xs_sorted", (SLOTS, E), F32, kind="Internal").ap()
        ys_sorted = nc.dram_tensor("ys_sorted", (SLOTS, E), F32, kind="Internal").ap()

        def sorted_rows(rows, j):
            return rows.rearrange("(j p) c -> j p c", p=P)[j]

        sA = bank("sA", 2)
        sB = bank("sB", 2)
        tp = [bank("tp0"), bank("tp1")]
        b6 = bank("b6")
        b7 = bank("b7")

        ident = cst[:, C_IDENT:C_IDENT + P]

        def flat(ap):
            names = "abcdef"[:len(ap.shape) - 1]
            return ap.rearrange(f"p {' '.join(names)} -> p ({' '.join(names)})")

        d_wq, d_cst, d_wo, d_wrt, d_small, d_x, d_kx, d_vn, d_ffn, d_shared = (sem(s) for s in (
            "d_wq", "d_cst", "d_wo", "d_wrt", "d_small", "d_x", "d_kx", "d_vn", "d_ffn", "d_shared"))
        d_zero, hot_zeroed = sem("d_zero"), sem("hot_zeroed")
        d_xT = [sem("d_xT0"), sem("d_xT1")]
        d_kbd = [sem("d_kbd0"), sem("d_kbd1")]
        d_disp = sem("d_disp")
        passed = sem("passed")
        d_xe = [sem(f"d_xe{i}") for i in range(2)]
        d_ye = [sem(f"d_ye{i}") for i in range(2)]
        d_yg = [sem(f"d_yg{i}") for i in range(TILES)]
        d_out = sem("d_out")
        kbd_zeroed, vbd_zeroed, kx_zeroed, vx_zeroed, zero_ok = (sem(s) for s in (
            "kbd_zeroed", "vbd_zeroed", "kx_zeroed", "vx_zeroed", "zero_ok"))
        fuse_mm, fuse_wk, fuse_wv, k0_mm, msk_ok = (sem(s) for s in (
            "fuse_mm", "fuse_wk", "fuse_wv", "k0_mm", "msk_ok"))
        names = """qk_mm v_mm q_cp k_cp v_cp s1_mm m1_ok sub1 exp1 sum1 rec1 nrm1
        pt1a_mm pt1b_mm pt1a_cp pt1b_cp c_mm c_cp o1_mm res1_ok st1_ok mv1_ok va1_ok rs1_ok x1_ok
        qx_mm qx_cp s2a_mm s2b_mm m2a m2b sub2a sub2b exp2a exp2b pt2_mm0 pt2_mm1 pt2_mm2 pt2_mm3
        pt2_cp0 pt2_cp1 pt2_cp2 pt2_cp3 vx_half vx_ok o2_mm o2_cp ot_mm rl2_ok a2_ok res2_ok st2_ok
        mv2_ok va2_ok rs2_ok x2_ok x2T_mm x2T_cp lg_mm top_ok topi_ok topf_ok hot_ok sct_ok score_ok
        x2_kept x2T_kept xs_ok rank_mm route ebi_ok pos_ok
        xeT_mm xeT_cp gu_mm th_ok gt_ok hid_ok hT_mm hT_cp dn_mm z_ok ye_ok
        res3_ok st3_ok mv3_ok va3_ok rs3_ok shift_ok fin0_ok fin1_ok fin2_ok""".split()
        S = {name: sem(name) for name in names}

        def after(eng, name, count):
            if isinstance(count, int) and count <= 0:
                return
            eng.wait_ge(S[name], count)

        def after_alone(eng, name, count):
            after(eng, name, count)
            eng.sem_inc(passed, 1)

        def steps(eng, step, last_steps):
            for n in range(3):
                step(n, n % 2, n // 2, n >= 1, n >= 2, False, n >= 1)
            with eng.Fori(1, TILES // 2 - 1) as it:
                step(2 * it + 1, 1, it, True, True, True, True)
                step(2 * it + 2, 0, it + 1, True, True, True, True)
            step(TILES - 1, 1, TILES // 2 - 1, True, True, True, False)
            last_steps()

        block = stack.enter_context(nc.Block())

        @block.sync
        def _(sp):
            sp.dma_start(wsm[:, :, :], w_small).then_inc(d_small, 16)
            sp.dma_start(xTt[:, 0, :, :], xT[0]).then_inc(d_xT[0], 16)
            sp.dma_start(wq[:, :, :], w_q).then_inc(d_wq, 16)
            sp.dma_start(cst[:, :], consts).then_inc(d_cst, 16)
            sp.dma_start(xTt[:, 1, :, :], xT[1]).then_inc(d_xT[1], 16)

            def diagonal(p):
                for h in range(HG):
                    sp.dma_start(kbd[D * h:D * h + D, p, :, :, T * h:T * h + T],
                                 kT[D * h:D * h + D, p, :, :, :]).then_inc(d_kbd[p], 16)

            def load(n, p):
                after_alone(sp, "k_cp", n + 1)
                after_alone(sp, "s1_mm", n - 1)
                diagonal(p)

            def load_xT(n, p):
                after_alone(sp, "v_mm", n + 1)
                sp.dma_start(xTt[:, p, :, :], xT[n + 2]).then_inc(d_xT[p], 16)

            def load_kx(b):
                for kv in range(XKV):
                    r = CX * b + XD * kv
                    sp.dma_start(kx[r:r + XD, :, b, T * kv:T * kv + T], ctx_k[b, kv]).then_inc(d_kx, 16)

            sp.wait_ge(kbd_zeroed, 1)
            load(0, 0)
            sp.wait_ge(kbd_zeroed, 2)
            load(1, 1)
            sp.dma_start(wo[:, :, :], w_out).then_inc(d_wo, 16)
            sp.dma_start(x_all[:, :, :], x.rearrange("t p c -> p t c")).then_inc(d_x, 16)
            load_xT(0, 0)
            sp.wait_ge(kx_zeroed, 2)
            for b in range(2):
                load_kx(b)
            sp.dma_start(wrt[:, :, :], router).then_inc(d_wrt, 16)
            load_xT(1, 1)
            for half in range(2):
                sp.dma_start(vnat[64 * half:64 * half + 64, :, :], ctx_v.rearrange("b s c -> s b c")).then_inc(d_vn, 16)
            sp.dma_start(wff[:, NE, :], w_ffn[NE]).then_inc(d_shared, 16)
            with sp.Fori(1, TILES // 2 - 1) as it:
                for p in range(2):
                    load(2 * it + p, p)
                    load_xT(2 * it + p, p)
                    e = 2 * (2 * it + p) - 4
                    sp.dma_start(wff[:, bass.ds(e, 2), :],
                                 w_ffn[bass.ds(e, 2)].rearrange("e p w -> p e w")).then_inc(d_ffn, 16)
            for n in range(TILES - 2, TILES):
                load(n, n % 2)

            sp.wait_ge(d_disp, 16 * TILES)

            def load_block(j, p):
                after_alone(sp, "xeT_mm", j - 1)
                sp.dma_start(xe[:, p, :], sorted_rows(xs_sorted, j)).then_inc(d_xe[p], 16)

            def store_block(j, p):
                after_alone(sp, "ye_ok", j + 1)
                sp.dma_start(sorted_rows(ys_sorted, j), ye[:, p, :]).then_inc(d_ye[p], 16)

            for e in range(5):
                load_block(e, e % 2)
            with sp.Fori(2, BLOCKS // 2) as it:
                for p in range(2):
                    load_block(2 * it + 1 + p, 1 - p)
                    store_block(2 * it + p - 4, p)
            for e in range(BLOCKS - 5, BLOCKS):
                store_block(e, e % 2)
            for g, (a, z) in enumerate(LAST_GROUPS):
                for t in range(a, z, 2):
                    after(sp, f"fin{g}_ok", t - a + 2)
                    sp.dma_start(out[t:t + 2].rearrange("t p c -> p t c"), fin[:, t:t + 2, :]).then_inc(d_out, 16)
            sp.wait_ge(d_out, 16 * TILES // 2)

        @block.gpsimd
        def _(pool):
            pool.memset(kbd[:, 0, :, :, :], 0.0).then_inc(kbd_zeroed, 1)
            pool.memset(kx[:, 0:TILES // 2, :, :], 0.0).then_inc(kx_zeroed, 1)
            pool.memset(kbd[:, 1, :, :, :], 0.0).then_inc(kbd_zeroed, 1)
            pool.memset(vx[:, :, :, :, :, :], 0.0).then_inc(vx_zeroed, 1)
            pool.wait_ge(vx_zeroed, 1)
            for kv in range(2):
                pool.memset(vx[64 * kv:64 * kv + 64, :, :, :, kv, XD:XD + 1], 1.0).then_inc(vx_zeroed, 1)
                pool.wait_ge(vx_zeroed, 2 + kv)
            pool.wait_ge(d_cst, 16)

            def context_values(t, p):
                if isinstance(t, int) and t == 0:
                    pool.wait_ge(d_vn, 32)
                for kv in range(2):
                    rows = slice(64 * kv, 64 * kv + 64)
                    src = vnat[rows, bass.ds(2 * t, 2), :].rearrange("p b (k v d) -> p b k v d", k=4, v=2)
                    name = ("vx_half", "vx_ok")[kv]
                    pool.tensor_copy(vx[rows, p, :, :, kv, 0:XD], src[:, :, :, kv, :]).then_inc(S[name], 1)
                    after(pool, name, t + 1)

            def inverse_deviation(t, i, va, rs):
                after(pool, f"va{i}_ok", t + 1)
                pool.tensor_tensor(rs[:, :], va[:, :], cst[:, C_POW:C_POW + 1], ALU.pow).then_inc(S[f"rs{i}_ok"], 1)

            def keep_rows(t, p):
                after(pool, "x2T_cp", t + 1)
                pool.tensor_copy(z_all[:, t, :], x2[:, p, :]).then_inc(S["x2_kept"], 1)
                pool.tensor_copy(x2T_all[:, t, :], flat(x2s[:, :, :])).then_inc(S["x2T_kept"], 1)

            def scored_rows(t, p):
                after(pool, "score_ok", t + 1)
                pool.tensor_tensor(xs[:, t, :], x2[:, p, :],
                                   score[:, p:p + 1].to_broadcast([P, E]), ALU.mult).then_inc(S["xs_ok"], 1)

            def step(n, p, half, do_cross, do_ffn, do_weigh, do_proj):
                if do_weigh:
                    scored_rows(n - 3, 1 - p)
                after(pool, "rec1", n + 1)
                after(pool, "pt1b_mm", n)
                pool.tensor_tensor(p1n[:, :, :], p1[:, :, :],
                                   r1[:, :].unsqueeze(2).to_broadcast([P, H, T]), ALU.mult).then_inc(S["nrm1"], 1)
                if isinstance(n, int) and n == 0:
                    pool.wait_ge(zero_ok, 1)
                    pool.dma_start(xs_sorted.rearrange("(j p) c -> p j c", p=P),
                                   zero[:, :].unsqueeze(1).to_broadcast([P, BLOCKS, E])).then_inc(d_zero, 16)
                if do_cross:
                    context_values(n - 1, 1 - p)
                if do_ffn:
                    inverse_deviation(n - 2, 2, va2, rs2)
                    keep_rows(n - 2, p)
                inverse_deviation(n, 1, va1, rs1)

            def last_steps():
                scored_rows(TILES - 3, 1)
                context_values(TILES - 1, 1)
                a, z = TILES - 2, TILES - 1
                inverse_deviation(a, 2, va2, rs2)
                keep_rows(a, 0)
                inverse_deviation(z, 2, va2, rs2)
                scored_rows(a, 0)
                keep_rows(z, 1)
                scored_rows(z, 1)

            steps(pool, step, last_steps)

            after(pool, "xs_ok", TILES)
            after(pool, "pos_ok", 1)
            pool.wait_ge(d_zero, 16)
            for t in range(TILES):
                pool.indirect_dma_start(xs_sorted, bass.IndirectOffsetOnAxis(pos[:, t:t + 1], 0),
                                        xs[:, t, :], None).then_inc(d_disp, 16)
            pool.wait_ge(d_ye[0], 16 * ((BLOCKS + 1) // 2))
            pool.wait_ge(d_ye[1], 16 * (BLOCKS // 2))
            for t in range(TILES):
                pool.indirect_dma_start(yg[:, t, :], None, ys_sorted,
                                        bass.IndirectOffsetOnAxis(pos[:, t:t + 1], 0)).then_inc(d_yg[t], 16)
            for a, z in LAST_GROUPS:
                after(pool, "va3_ok", z)
                pool.tensor_tensor(rs3[:, a:z], va3[:, a:z], cst[:, C_POW:C_POW + 1].to_broadcast([P, z - a]),
                                   ALU.pow).then_inc(S["rs3_ok"], 1)

        @block.tensor
        def _(pe):
            def mm(o, lhsT, rhs, start=True, stop=True, **k):
                return pe.matmul(o, lhsT, rhs, start=start, stop=stop, **k)

            pe.wait_ge(d_small, 16)
            for w in range(2):
                for k in range(KC):
                    last = mm(sB[:, 512 * w + E * k:512 * w + E * k + E], wsm[:, w, P * k:P * k + P], wsm[:, 2 + w, :])
                last.then_inc(fuse_mm, 1)

            def values(t, p):
                if isinstance(t, int) and t == 0:
                    pe.wait_ge(fuse_wv, 1)
                for par in range(2):
                    for s in range(2):
                        for k in range(KC):
                            last = mm(tp[1][64 * par:64 * par + 64, P * s:P * s + P], xTt[:, p, k, T * s:T * s + T],
                                      wv[:, k, par, :], start=(k == 0), stop=(k == KC - 1))
                last.then_inc(S["v_mm"], 1)

            def project(weight, p, o):
                for g in range(2):
                    for k in range(KC):
                        last = mm(o[:, P * g:P * g + P], weight[:, k, P * g:P * g + P],
                                  xTt[:, p, k, :], start=(k == 0), stop=(k == KC - 1))
                return last

            def queries_keys(t, half, p):
                pe.wait_ge(d_xT[p], 16 * half + 16)
                project(wq, p, tp[0][:, 0:E])
                project(wk, p, tp[0][:, E:2 * E]).then_inc(S["qk_mm"], 1)

            pe.wait_ge(d_xT[0], 16)
            pe.wait_ge(fuse_wk, 1)
            project(wk, 0, sA[:, 0:E]).then_inc(k0_mm, 1)
            pe.wait_ge(d_wq, 16)
            project(wq, 0, tp[0][:, 0:E]).then_inc(S["qk_mm"], 1)
            values(0, 0)
            after(pe, "q_cp", 1)
            queries_keys(1, 0, 1)
            after(pe, "v_cp", 1)
            values(1, 1)
            pe.wait_ge(d_cst, 16)
            pe.wait_ge(msk_ok, 1)

            def self_scores(t, p, half):
                after(pe, "q_cp", t + 1)
                pe.wait_ge(d_kbd[p], 16 * HG * (half + 1))
                after(pe, "sub2b", t - 1)
                if isinstance(t, int) and t == 1:
                    after(pe, "sub1", 1)
                for g in range(2):
                    for s in range(2):
                        o = sA[T * s:T * s + T, 512 * g:512 * g + 512]
                        mm(o, msk[:, M_IDENT + T * s:M_IDENT + T * s + T], msk[:, M_CAUSAL:M_CAUSAL + 512], stop=False)
                        last = mm(o, qT[:, p, g, T * s:T * s + T], kbd[:, p, g, s, :], start=False)
                last.then_inc(S["s1_mm"], 1)

            def cross_output(t, p):
                after(pe, "pt2_cp3", t + 1)
                after(pe, "vx_ok", t + 1)
                if not isinstance(t, int) or t < TILES - 1:
                    after(pe, "res1_ok", t + 2)
                else:
                    after(pe, "o2_cp", t)
                for s in range(2):
                    for kp in range(4):
                        last = mm(b7[32 * kp:32 * kp + 32, 256 * s:256 * s + 256], flat(vx[:, p, s, kp, :, :]),
                                  flat(p2T[:, s, kp, :, :]))
                last.then_inc(S["o2_mm"], 1)

            def cross_queries(t, p):
                after(pe, "x1_ok", t + 1)
                after(pe, "topi_ok", t - 1)
                x1v = x1[:, p, :].rearrange("p (g c) -> p g c", g=XG)
                for s in range(2):
                    for g in range(XG):
                        last = mm(b6[64 * s:64 * s + 64, T * g:T * g + T], x1v[:, g, :],
                                  cst[:, C_IDENT + T * s:C_IDENT + T * s + T])
                last.then_inc(S["qx_mm"], 1)

            def cross_output_back(t, bank_=b6):
                after(pe, "o2_cp", t + 1)
                if not isinstance(t, int) or t < TILES - 1:
                    after(pe, "qx_cp", t + 2)
                for g in range(XG):
                    last = pe.transpose(bank_[:, P * g:P * g + P], flat(oT[:, g, :, :]), ident)
                last.then_inc(S["ot_mm"], 1)

            def cross_scores(t, gp):
                after(pe, "qx_cp", t + 1)
                if gp == 0:
                    after(pe, "sub2a", t)
                elif isinstance(t, int) and t == TILES - 1:
                    after(pe, "sub2b", t)
                    after(pe, "hid_ok", 1)
                else:
                    after(pe, "sub1", t + 2)
                if isinstance(t, int) and t == 0 and gp == 0:
                    pe.wait_ge(d_kx, 16 * 2 * XKV)
                for s in range(2):
                    last = mm((sB, sA)[gp][:, 512 * s:512 * s + 512], flat(qx[:, 2 * gp:2 * gp + 2, :]), kx[:, t, s, :])
                last.then_inc(S[("s2a_mm", "s2b_mm")[gp]], 1)

            def transpose_x2(t, p):
                after(pe, "x2_ok", t + 1)
                if isinstance(t, int) and t == TILES - 1:
                    after(pe, "topi_ok", t)
                for k in range(KC):
                    last = pe.transpose(b6[:, P * k:P * k + P], x2[:, p, P * k:P * k + P], ident)
                last.then_inc(S["x2T_mm"], 1)

            def logits(t):
                if isinstance(t, int) and t == 0:
                    pe.wait_ge(d_wrt, 16)
                after(pe, "x2T_cp", t + 1)
                for k in range(KC):
                    last = mm(b6[:, 256:256 + NE], x2s[:, k, :], wrt[:, k, :], start=(k == 0), stop=(k == KC - 1))
                last.then_inc(S["lg_mm"], 1)

            def transpose_self(t, projected):
                after(pe, "nrm1", t + 1)
                for c, bank_ in enumerate(tp):
                    if projected:
                        after(pe, ("q_cp", "v_cp")[c], t + 2)
                    else:
                        after(pe, ("pt2_cp2", "pt2_cp3")[c], t - 1)
                    for i in range(4):
                        hp = 4 * c + i
                        last = pe.transpose(bank_[:, P * i:P * i + P], flat(p1n[:, 2 * hp:2 * hp + 2, :]), ident)
                    last.then_inc(S[("pt1a_mm", "pt1b_mm")[c]], 1)

            def self_output(t, p):
                after(pe, "pt1b_cp", t + 1)
                after(pe, "v_cp", t + 1)
                after(pe, "o2_cp", t - 1)
                for s in range(2):
                    for hp in range(8):
                        r = 32 * (hp % 4)
                        last = mm(b7[r:r + 32, P * (hp // 4) + T * s:P * (hp // 4) + T * s + T],
                                  vbd[:, p, s, hp, :], p1T[:, hp, T * s:T * s + T])
                last.then_inc(S["c_mm"], 1)

            def project_out(t):
                if isinstance(t, int) and t == 0:
                    pe.wait_ge(d_wo, 16)
                after(pe, "c_cp", t + 1)
                for g in range(KC):
                    last = mm(b7[:, 0:E], cT[:, g, :], wo[:, g, :], start=(g == 0), stop=(g == KC - 1))
                last.then_inc(S["o1_mm"], 1)

            def transpose_cross(t, gp):
                after(pe, ("exp2a", "exp2b")[gp], t + 1)
                for s in range(2):
                    if gp == 1:
                        after(pe, f"pt2_cp{s}", t + 1)
                    elif isinstance(t, int) and t == TILES - 1:
                        after(pe, f"pt2_cp{2 + s}", t)
                    else:
                        after(pe, ("pt1a_cp", "pt1b_cp")[s], t + 2)
                    for i in range(4):
                        last = pe.transpose(tp[s][:, P * i:P * i + P],
                                            flat(p2[:, gp, XKV * s + 2 * i:XKV * s + 2 * i + 2, :]), ident)
                    last.then_inc(S[f"pt2_mm{2 * gp + s}"], 1)

            def step(n, p, half, do_cross, do_ffn, do_weigh, do_proj):
                q = 1 - p
                if not isinstance(n, int) or n != 1:
                    self_scores(n, p, half)
                if isinstance(n, int) and n == 0:
                    self_scores(1, 1, 0)
                if do_ffn:
                    transpose_cross(n - 2, 1)
                if do_cross:
                    cross_queries(n - 1, q)
                if do_proj and not (isinstance(n, int) and n == 1):
                    after(pe, "pt2_cp2", n - 1)
                    queries_keys(n + 1, half + p, q)
                if do_cross:
                    cross_scores(n - 1, 0)
                if do_ffn:
                    cross_output(n - 2, p)
                if do_proj:
                    after(pe, "pt2_cp3", n - 1)
                    values(n + 1, q)
                if do_ffn:
                    cross_output_back(n - 2)
                transpose_self(n, not isinstance(n, int) or n < TILES - 1)
                if do_cross:
                    cross_scores(n - 1, 1)
                self_output(n, p)
                if do_cross:
                    transpose_cross(n - 1, 0)
                if do_ffn:
                    transpose_x2(n - 2, p)
                project_out(n)
                if isinstance(n, int) and n == 0:
                    queries_keys(2, 1, 0)
                if do_ffn:
                    logits(n - 2)

            def rows_of(e, p, half):
                pe.wait_ge(d_xe[p], 16 * (half + 1))
                for k in range(KC):
                    last = pe.transpose(tp[p][:, P * k:P * k + P], xe[:, p, P * k:P * k + P], ident)
                last.then_inc(S["xeT_mm"], 1)

            def up(j, p, rows, weights):
                for k in range(KC):
                    last = mm(sA[:, 512 * p:512 * p + 512], rows(k), weights(2 * F * k, 2 * F),
                              start=(k == 0), stop=(k == KC - 1))
                last.then_inc(S["gu_mm"], 1)

            def transpose_hidden(j, p):
                after(pe, "hid_ok", j + 1)
                for k in range(KC):
                    last = pe.transpose(sB[:, 512 * p + P * k:512 * p + P * k + P], hid[:, p, P * k:P * k + P], ident)
                last.then_inc(S["hT_mm"], 1)

            def down(j, p, weights):
                after(pe, "hT_cp", j + 1)
                for k in range(KC):
                    last = mm(sB[:, 512 * p + E:512 * p + 2 * E], hT[:, p, k, :], weights(KC * 2 * F + E * k, E),
                              start=(k == 0), stop=(k == KC - 1))
                last.then_inc(S["dn_mm"], 1)

            def shared(c, n):
                return wff[:, NE, c:c + n]

            def expert_of(e):
                chosen = pe.value_load(ebi[0:1, bass.ds(e, 1)], min_val=0, max_val=NE - 1)
                return lambda c, n: flat(wff[:, bass.ds(chosen, 1), c:c + n])

            def shared_up(j):
                after(pe, "x2T_kept", j + 1)
                up(j, j % 2, lambda k: x2T_all[:, j, P * k:P * k + P], shared)

            def shared_turn(j):
                p = j % 2
                if j >= 2:
                    after(pe, "z_ok", j - 3)
                    transpose_hidden(j - 2, p)
                shared_up(j)
                if j >= 2:
                    down(j - 2, p, shared)

            def last_steps():
                a, z = TILES - 2, TILES - 1
                transpose_cross(a, 1)
                pe.wait_ge(d_shared, 16)
                after(pe, "sub2b", z)
                shared_up(0)
                cross_queries(z, 1)
                cross_output(a, 0)
                cross_scores(z, 0)
                cross_scores(z, 1)
                cross_output_back(a)
                transpose_cross(z, 0)
                transpose_hidden(0, 0)
                down(0, 0, shared)
                transpose_cross(z, 1)
                shared_up(1)
                transpose_x2(a, 0)
                cross_output(z, 1)
                transpose_hidden(1, 1)
                logits(a)
                cross_output_back(z, tp[0])
                shared_up(2)
                down(1, 1, shared)
                after(pe, "z_ok", 1)
                transpose_hidden(2, 0)
                transpose_x2(z, 1)
                logits(z)
                down(2, 0, shared)
                after(pe, "hot_ok", TILES)
                pe.wait_ge(hot_zeroed, 1)
                pe.wait_ge(msk_ok, 2)
                for k in range(TILES + 1):
                    c = M_ONES if k else M_RANK
                    last = mm(b6[:, 0:(TILES + 1) * NE], msk[:, c:c + P], flat(onehot[:, TILES - k:2 * TILES + 1 - k, :]),
                              start=(k == 0), stop=(k == TILES))
                last.then_inc(S["rank_mm"], 1)
                shared_up(3)
                shared_up(4)
                for j in range(5, TILES):
                    shared_turn(j)

            steps(pe, step, last_steps)

            pe.wait_ge(d_ffn, 16 * NE // 2)
            after(pe, "ebi_ok", 1)

            def expert_turn(e, p, half):
                if isinstance(e, int) and e < 4:
                    after(pe, "z_ok", TILES + e - 3)
                else:
                    after(pe, "ye_ok", e - 3)
                transpose_hidden(TILES + e - 2, p)
                rows_of(e + 1, 1 - p, half)
                weights_up = expert_of(e)
                if isinstance(e, int) and e < 2:
                    weights_down = shared
                else:
                    weights_down = expert_of(e - 2)
                after(pe, "xeT_cp", e + 1)
                up(TILES + e, p, lambda k: xeT[:, p, k, :], weights_up)
                down(TILES + e - 2, p, weights_down)

            rows_of(0, 0, 0)
            for e in range(4):
                expert_turn(e, e % 2, (e + 1) // 2)
            with pe.Fori(2, BLOCKS // 2) as it:
                for p in range(2):
                    expert_turn(2 * it + p, p, it + p)
            e = BLOCKS - 1
            for i in (e - 2, e - 1):
                after(pe, "ye_ok", i - 1)
                transpose_hidden(TILES + i, i % 2)
                if i == e - 2:
                    chosen = expert_of(e)
                    after(pe, "xeT_cp", e + 1)
                    up(TILES + e, 0, lambda k: xeT[:, 0, k, :], chosen)
            for i in (e - 2, e - 1):
                down(TILES + i, i % 2, expert_of(i))
            after(pe, "ye_ok", e - 1)
            transpose_hidden(TILES + e, 0)
            down(TILES + e, 0, expert_of(e))

        @block.scalar
        def _(act):
            act.wait_ge(fuse_mm, 1)
            act.copy(flat(wk[:, :, :]), sB[:, 0:512]).then_inc(fuse_wk, 1)

            def copy_qk(t, p):
                if isinstance(t, int) and t == 0:
                    act.wait_ge(k0_mm, 1)
                    act.copy(flat(kT[:, p, :, :, :]), sA[:, 0:E]).then_inc(S["k_cp"], 1)
                    after(act, "qk_mm", 1)
                else:
                    after(act, "qk_mm", t + 1)
                    act.copy(flat(kT[:, p, :, :, :]), tp[0][:, E:2 * E]).then_inc(S["k_cp"], 1)
                act.mul(flat(qT[:, p, :, :]), tp[0][:, 0:E], SELF_SCALE).then_inc(S["q_cp"], 1)

            def copy_v(t, p):
                after(act, "v_mm", t + 1)
                after(act, "c_mm", t - 1)
                for par in range(2):
                    rows = slice(64 * par, 64 * par + 64)
                    last = act.copy(vbd[rows, p, :, :, D * par:D * par + D],
                                    tp[1][rows, 0:E].rearrange("p (s h d) -> p s h d", s=2, h=8))
                last.then_inc(S["v_cp"], 1)

            copy_qk(0, 0)
            act.wait_ge(vbd_zeroed, 1)
            copy_v(0, 0)
            act.wait_ge(d_cst, 16)
            act.copy(msk[:, M_IDENT:M_IDENT + P], ident)
            act.copy(msk[:, M_CAUSAL:M_CAUSAL + 512].rearrange("p (h s) -> p h s", h=HG),
                     cst[:, C_CAUSAL:C_CAUSAL + T].unsqueeze(1).to_broadcast([P, HG, T])).then_inc(msk_ok, 1)
            act.copy(msk[:, M_RANK:M_RANK + P], cst[:, C_RANK:C_RANK + P]).then_inc(msk_ok, 1)
            copy_qk(1, 1)
            copy_v(1, 1)

            def copy_cross_output(t):
                after(act, "o2_mm", t + 1)
                act.copy(oT[:, :, :, :], b7[:, :].rearrange("p (s g t) -> p g s t", s=2, g=XG)).then_inc(S["o2_cp"], 1)

            def copy_cross_queries(t):
                after(act, "qx_mm", t + 1)
                act.mul(flat(qx[:, :, :]), b6[:, 0:E], CROSS_SCALE).then_inc(S["qx_cp"], 1)

            def copy_x2(t):
                after(act, "x2T_mm", t + 1)
                act.copy(flat(x2s[:, :, :]), b6[:, 0:E]).then_inc(S["x2T_cp"], 1)

            def exp_cross(t, gp):
                after(act, ("sub2a", "sub2b")[gp], t + 1)
                act.activation(p2[:, gp, :, :], p2[:, gp, :, :], ACT.Exp).then_inc(S[("exp2a", "exp2b")[gp]], 1)

            def tanh_score(t):
                after(act, "top_ok", t + 1)
                act.activation(sc_t[:, :], top[:, 0:1], ACT.Tanh, scale=0.5).then_inc(S["sct_ok"], 1)

            def copy_cross_probs(t, gp):
                after(act, "o2_mm", t)
                for s in range(2):
                    after(act, f"pt2_mm{2 * gp + s}", t + 1)
                    act.copy(p2T[:, s, :, gp, :], tp[s][:, :].rearrange("p (k t) -> p k t", k=4)).then_inc(
                        S[f"pt2_cp{2 * gp + s}"], 1)

            def step(n, p, half, do_cross, do_ffn, do_weigh, do_proj):
                if do_ffn:
                    copy_cross_probs(n - 2, 1)
                if do_cross:
                    copy_cross_queries(n - 1)
                after(act, "sub1", n + 1)
                act.activation(p1[:, :, :], p1[:, :, :], ACT.Exp).then_inc(S["exp1"], 1)
                if do_proj:
                    copy_qk(n + 1, 1 - p)
                if do_ffn:
                    copy_cross_output(n - 2)
                if do_proj:
                    copy_v(n + 1, 1 - p)
                if do_cross:
                    exp_cross(n - 1, 0)
                for c in range(2):
                    after(act, ("pt1a_mm", "pt1b_mm")[c], n + 1)
                    after(act, "c_mm", n)
                    act.copy(flat(p1T[:, 4 * c:4 * c + 4, :]), tp[c][:, :]).then_inc(S[("pt1a_cp", "pt1b_cp")[c]], 1)
                after(act, "c_mm", n + 1)
                act.copy(flat(cT[:, :, :]), b7[:, 0:E]).then_inc(S["c_cp"], 1)
                if do_cross:
                    copy_cross_probs(n - 1, 0)
                if do_ffn:
                    copy_x2(n - 2)
                if do_cross:
                    exp_cross(n - 1, 1)
                if do_ffn:
                    tanh_score(n - 2)

            def copy_rows(e, p):
                after(act, "xeT_mm", e + 1)
                after(act, "gu_mm", TILES + e - 1)
                act.copy(flat(xeT[:, p, :, :]), tp[p][:, 0:E]).then_inc(S["xeT_cp"], 1)

            def tanh_gate(j, p):
                after(act, "gu_mm", j + 1)
                after(act, "gt_ok", j - 1)
                act.activation(th[:, p, :], sA[:, 512 * p:512 * p + F], ACT.Tanh, scale=0.5).then_inc(S["th_ok"], 1)

            def copy_hidden(j, p):
                after(act, "hT_mm", j + 1)
                after(act, "dn_mm", j - 1)
                act.copy(flat(hT[:, p, :, :]), sB[:, 512 * p:512 * p + E]).then_inc(S["hT_cp"], 1)

            def copy_result(e, p, stored):
                after(act, "dn_mm", TILES + e + 1)
                if not isinstance(stored, int) or stored > 0:
                    act.wait_ge(d_ye[p], 16 * stored)
                act.copy(ye[:, p, :], sB[:, 512 * p + E:512 * p + 2 * E]).then_inc(S["ye_ok"], 1)

            def shared_turn(j):
                if j >= 2:
                    copy_hidden(j - 2, j % 2)
                tanh_gate(j, j % 2)

            def last_steps():
                a, z = TILES - 2, TILES - 1
                copy_cross_probs(a, 1)
                tanh_gate(0, 0)
                copy_cross_queries(z)
                copy_cross_output(a)
                exp_cross(z, 0)
                copy_cross_probs(z, 0)
                copy_hidden(0, 0)
                exp_cross(z, 1)
                copy_cross_probs(z, 1)
                tanh_gate(1, 1)
                copy_x2(a)
                copy_cross_output(z)
                copy_hidden(1, 1)
                tanh_gate(2, 0)
                tanh_score(a)
                copy_x2(z)
                copy_hidden(2, 0)
                tanh_score(z)
                tanh_gate(3, 1)
                tanh_gate(4, 0)
                for j in range(5, TILES):
                    shared_turn(j)

            steps(act, step, last_steps)

            def expert_turn(e, p, stored):
                copy_hidden(TILES + e - 2, p)
                copy_rows(e + 1, 1 - p)
                tanh_gate(TILES + e, p)
                if not isinstance(e, int) or e >= 2:
                    copy_result(e - 2, p, stored)

            copy_rows(0, 0)
            for e in range(4):
                expert_turn(e, e % 2, 0)
            with act.Fori(2, BLOCKS // 2) as it:
                for p in range(2):
                    expert_turn(2 * it + p, p, it - 1)
            e = BLOCKS - 1
            copy_hidden(TILES + e - 2, 0)
            tanh_gate(TILES + e, 0)
            copy_hidden(TILES + e - 1, 1)
            copy_result(e - 2, 0, BLOCKS // 2 - 1)
            copy_result(e - 1, 1, BLOCKS // 2 - 1)
            copy_hidden(TILES + e, 0)
            copy_result(e, 0, BLOCKS // 2)

            after(act, "shift_ok", 1)
            for t in range(*LAST_GROUPS[0]):
                act.activation(fin[:, t, :], res3[:, t, :], ACT.Identity, bias=shift3[:, t:t + 1],
                               scale=rs3[:, t:t + 1]).then_inc(S["fin0_ok"], 1)

        @block.vector
        def _(dve):
            dve.memset(zero[:, :], 0.0).then_inc(zero_ok, 1)
            dve.memset(msk[:, M_ONES:M_ONES + P], 1.0)
            dve.memset(onehot[:, 0:TILES, :], 0.0)
            dve.memset(onehot[:, 2 * TILES:, :], 0.0).then_inc(hot_zeroed, 1)
            dve.memset(vbd[:, :, :, :, :], 0.0).then_inc(vbd_zeroed, 1)
            dve.memset(kx[:, TILES // 2:TILES, :, :], 0.0).then_inc(kx_zeroed, 1)
            dve.wait_ge(fuse_mm, 2)
            dve.tensor_copy(flat(wv[:, :, :, :]), sB[:, 512:1024]).then_inc(fuse_wv, 1)

            def norm(t, src, stats, mv, va, i):
                dve.bn_stats(stats, src).then_inc(S[f"st{i}_ok"], 1)
                after_alone(dve, f"st{i}_ok", t + 1)
                dve.bn_aggr(mv, stats).then_inc(S[f"mv{i}_ok"], 1)
                after(dve, f"mv{i}_ok", t + 1)
                dve.tensor_scalar(va, mv[:, 1:2], EPS, None, ALU.add).then_inc(S[f"va{i}_ok"], 1)

            def cross_norm(t, p, bank_=b6):
                after(dve, "ot_mm", t + 1)
                o = bank_[:, :].rearrange("p (g k e) -> p g k e", g=XG, k=XKV)
                dve.reciprocal(rl2[:, :, :], o[:, :, :, XD]).then_inc(S["rl2_ok"], 1)
                after(dve, "rl2_ok", t + 1)
                dve.tensor_tensor(a2[:, :].rearrange("p (g k d) -> p g k d", g=XG, k=XKV), o[:, :, :, 0:XD],
                                  rl2[:, :, :].unsqueeze(3).to_broadcast([P, XG, XKV, XD]), ALU.mult).then_inc(S["a2_ok"], 1)
                after(dve, "a2_ok", t + 1)
                dve.tensor_tensor(res2[:, :], a2[:, :], x1[:, p, :], ALU.add).then_inc(S["res2_ok"], 1)
                after(dve, "res2_ok", t + 1)
                norm(t, res2[:, :], st2[:, :], mv2[:, :], va2[:, :], 2)

            def cross_normed(t, p):
                after(dve, "rs2_ok", t + 1)
                dve.tensor_scalar(x2[:, p, :], res2[:, :], mv2[:, 0:1], rs2[:, 0:1],
                                  ALU.subtract, ALU.mult).then_inc(S["x2_ok"], 1)

            def cross_max(t, gp):
                after(dve, ("s2a_mm", "s2b_mm")[gp], t + 1)
                s2 = (sB, sA)[gp][:, :].rearrange("p (k s) -> p k s", k=2 * XKV)
                dve.tensor_reduce(m2[:, gp, :], s2, AX, ALU.max).then_inc(S[("m2a", "m2b")[gp]], 1)

            def cross_sub(t, gp):
                s2 = (sB, sA)[gp][:, :].rearrange("p (k s) -> p k s", k=2 * XKV)
                name = "ab"[gp]
                after(dve, f"m2{name}", t + 1)
                after(dve, f"pt2_mm{2 * gp + 1}", t)
                dve.tensor_tensor(p2[:, gp, :, :], s2, m2[:, gp, :].unsqueeze(2).to_broadcast([P, 2 * XKV, T]),
                                  ALU.subtract).then_inc(S[f"sub2{name}"], 1)

            def choose(t):
                after_alone(dve, "lg_mm", t + 1)
                dve.max(top[:, :], b6[:, 256:256 + NE]).then_inc(S["top_ok"], 1)
                after_alone(dve, "top_ok", t + 1)
                dve.max_index(topi[:, :], top[:, :], b6[:, 256:256 + NE]).then_inc(S["topi_ok"], 1)

            def weigh(t, p):
                after(dve, "topi_ok", t + 1)
                dve.tensor_copy(topf[:, :], topi[:, 0:1]).then_inc(S["topf_ok"], 1)
                after(dve, "topf_ok", t + 1)
                dve.tensor_scalar(onehot[:, TILES + t, :], cst[:, C_EXPERT:C_EXPERT + NE], topf[:, 0:1], None,
                                  ALU.is_equal).then_inc(S["hot_ok"], 1)
                after(dve, "sct_ok", t + 1)
                dve.tensor_scalar(score[:, p:p + 1], sc_t[:, :], 0.5, 0.5, ALU.mult, ALU.add).then_inc(S["score_ok"], 1)

            def step(n, p, half, do_cross, do_ffn, do_weigh, do_proj):
                after(dve, "s1_mm", n + 1)
                s1 = sA[:, :].rearrange("p (h s) -> p h s", h=H)
                dve.tensor_reduce(m1[:, :], s1, AX, ALU.max).then_inc(S["m1_ok"], 1)
                after(dve, "m1_ok", n + 1)
                after(dve, "nrm1", n)
                dve.tensor_tensor(p1[:, :, :], s1, m1[:, :].unsqueeze(2).to_broadcast([P, H, T]),
                                  ALU.subtract).then_inc(S["sub1"], 1)
                if do_weigh:
                    weigh(n - 3, 1 - p)
                after(dve, "exp1", n + 1)
                dve.tensor_reduce(l1[:, :], p1[:, :, :], AX, ALU.add).then_inc(S["sum1"], 1)
                after(dve, "sum1", n + 1)
                dve.reciprocal(r1[:, :], l1[:, :]).then_inc(S["rec1"], 1)
                if do_cross:
                    cross_max(n - 1, 0)
                    cross_sub(n - 1, 0)
                if do_ffn:
                    cross_norm(n - 2, p)
                if do_cross:
                    cross_max(n - 1, 1)
                if do_ffn:
                    cross_normed(n - 2, p)
                if do_cross:
                    cross_sub(n - 1, 1)
                if isinstance(n, int) and n == 0:
                    dve.wait_ge(d_x, 16)
                after(dve, "o1_mm", n + 1)
                dve.tensor_tensor(res1[:, :], b7[:, 0:E], x_all[:, n, :], ALU.add).then_inc(S["res1_ok"], 1)
                after(dve, "res1_ok", n + 1)
                norm(n, res1[:, :], st1[:, :], mv1[:, :], va1[:, :], 1)
                if do_ffn:
                    choose(n - 2)
                after(dve, "rs1_ok", n + 1)
                after(dve, "res2_ok", n - 1)
                dve.tensor_scalar(x1[:, p, :], res1[:, :], mv1[:, 0:1], rs1[:, 0:1],
                                  ALU.subtract, ALU.mult).then_inc(S["x1_ok"], 1)

            def hidden(j, p):
                g = sA[:, 512 * p:512 * p + F]
                u = sA[:, 512 * p + F:512 * p + 2 * F]
                after(dve, "th_ok", j + 1)
                dve.scalar_tensor_tensor(gt[:, p, :], th[:, p, :], 1.0, g, ALU.add, ALU.mult).then_inc(S["gt_ok"], 1)
                after(dve, "gt_ok", j + 1)
                after(dve, "hT_mm", j - 1)
                dve.scalar_tensor_tensor(hid[:, p, :], gt[:, p, :], 0.5, u, ALU.mult, ALU.mult).then_inc(S["hid_ok"], 1)

            def add_shared(t):
                after(dve, "dn_mm", t + 1)
                after(dve, "x2_kept", t + 1)
                dve.tensor_tensor(z_all[:, t, :], sB[:, 512 * (t % 2) + E:512 * (t % 2) + 2 * E], z_all[:, t, :], ALU.add).then_inc(S["z_ok"], 1)

            done = [0]

            def link(instruction):
                done[0] += 1
                instruction.then_inc(S["route"], 1)
                dve.wait_ge(S["route"], done[0])

            dve.wait_ge(d_cst, 16)

            def place_tokens():
                after(dve, "rank_mm", 1)
                count = b6[:, TILES * NE:(TILES + 1) * NE]
                link(dve.tensor_tensor(over[:, :, :], count.unsqueeze(2).to_broadcast([P, NE, 8]),
                                       cst[:, C_STEP:C_STEP + 8].unsqueeze(1).to_broadcast([P, NE, 8]), ALU.is_gt))
                link(dve.tensor_reduce(nb[:, :], over[:, :, :], AX, ALU.add))
                link(dve.tensor_tensor(bef[:, :, :], nb[:, :].unsqueeze(1).to_broadcast([P, NE, NE]),
                                       cst[:, C_BEFORE:C_BEFORE + NE * NE].rearrange("p (a b) -> p a b", a=NE), ALU.mult))
                link(dve.tensor_reduce(first[:, :], bef[:, :, :], AX, ALU.add))
                link(dve.tensor_tensor(slot[:, :, :], b6[:, 0:TILES * NE].rearrange("p (t e) -> p t e", t=TILES),
                                       first[:, :].unsqueeze(1).to_broadcast([P, TILES, NE]), ALU.add))
                link(dve.tensor_tensor(chosen_slot[:, :, :], slot[:, :, :], onehot[:, TILES:2 * TILES, :], ALU.mult))
                link(dve.tensor_reduce(posf[:, :], chosen_slot[:, :, :], AX, ALU.add))
                dve.tensor_copy(pos[:, :], posf[:, :]).then_inc(S["pos_ok"], 1)

            def assign_blocks():
                link(dve.scalar_tensor_tensor(bend[:, :], nb[:, :], float(P), first[:, :], ALU.mult, ALU.add))
                link(dve.tensor_tensor(ebc[:, :, :], bend[:, :].unsqueeze(1).to_broadcast([P, BLOCKS, NE]),
                                       cst[:, C_BLOCK:C_BLOCK + BLOCKS].unsqueeze(2).to_broadcast([P, BLOCKS, NE]), ALU.is_le))
                link(dve.tensor_reduce(ebf[:, :], ebc[:, :, :], AX, ALU.add))
                link(dve.tensor_scalar(ebm[:, :], ebf[:, :], float(NE - 1), None, ALU.min))
                dve.tensor_copy(ebi[:, :], ebm[:, :]).then_inc(S["ebi_ok"], 1)

            def last_steps():
                a, z = TILES - 2, TILES - 1
                weigh(a - 1, 1)
                hidden(0, 0)
                for gp in range(2):
                    cross_max(z, gp)
                    cross_sub(z, gp)
                cross_norm(a, 0)
                cross_normed(a, 0)
                hidden(1, 1)
                add_shared(0)
                choose(a)
                cross_norm(z, 1, tp[0])
                hidden(2, 0)
                cross_normed(z, 1)
                weigh(a, 0)
                choose(z)
                weigh(z, 1)
                add_shared(1)
                place_tokens()
                hidden(3, 1)
                hidden(4, 0)
                assign_blocks()
                add_shared(2)
                for j in range(5, TILES):
                    hidden(j, j % 2)
                    add_shared(j - 2)

            steps(dve, step, last_steps)

            for e in range(4):
                if e < 2:
                    add_shared(TILES + e - 2)
                hidden(TILES + e, e % 2)
            with dve.Fori(2, BLOCKS // 2) as it:
                for p in range(2):
                    hidden(TILES + 2 * it + p, p)
            hidden(TILES + BLOCKS - 1, 0)

            for i in range(TILES + 2):
                if i < TILES:
                    dve.wait_ge(d_yg[i], 16)
                    dve.tensor_tensor(res3[:, i, :], yg[:, i, :], z_all[:, i, :], ALU.add).then_inc(S["res3_ok"], 1)
                if 1 <= i <= TILES:
                    after_alone(dve, "st3_ok", i - 1)
                    if i >= 2:
                        dve.bn_aggr(mv3[:, i - 2, :], st3[:, i - 2, :]).then_inc(S["mv3_ok"], 1)
                    after(dve, "res3_ok", i)
                    dve.bn_stats(st3[:, i - 1, :], res3[:, i - 1, :]).then_inc(S["st3_ok"], 1)
                if i >= 2:
                    if i == TILES + 1:
                        after_alone(dve, "st3_ok", TILES)
                        dve.bn_aggr(mv3[:, i - 2, :], st3[:, i - 2, :]).then_inc(S["mv3_ok"], 1)
                    after(dve, "mv3_ok", i - 1)
                    dve.tensor_scalar(va3[:, i - 2:i - 1], mv3[:, i - 2, 1:2], EPS, None, ALU.add).then_inc(S["va3_ok"], 1)
                if i == TILES - 2:
                    a, z = LAST_GROUPS[0]
                    after(dve, "rs3_ok", 1)
                    dve.scalar_tensor_tensor(shift3[:, a:z], mv3[:, a:z, 0], -1.0, rs3[:, a:z],
                                             ALU.mult, ALU.mult).then_inc(S["shift_ok"], 1)
            for g, (a, z) in enumerate(LAST_GROUPS[1:], 1):
                after(dve, "rs3_ok", g + 1)
                for t in range(a, z):
                    dve.tensor_scalar(fin[:, t, :], res3[:, t, :], mv3[:, t, 0:1], rs3[:, t:t + 1],
                                      ALU.subtract, ALU.mult).then_inc(S[f"fin{g}_ok"], 1)


def channel_order():
    import numpy as np

    return np.arange(E).reshape(XKV, XG, XD).transpose(1, 0, 2).reshape(-1)


def natural_order(y):
    import numpy as np

    out = np.empty_like(y)
    out[..., channel_order()] = y
    return out


def decoder_layout(i):
    import numpy as np

    def rows(w):
        return w.reshape(-1, P, w.shape[1]).transpose(1, 0, 2)

    a = {k: np.asarray(v) for k, v in i.items()}
    x = a["x"].reshape(TILES, P, E)
    order = channel_order()
    ctx = a["ctx_512"]
    ffn = [np.concatenate([rows(np.concatenate([g, u], 1)[order]).reshape(P, -1), rows(d[:, order]).reshape(P, -1)], 1) for g, u, d in
           [(a["L0_ffn_gate_w"][e], a["L0_ffn_up_w"][e], a["L0_ffn_down_w"][e]) for e in range(NE)]
           + [(a["L0_ffn_shared_gate_w"], a["L0_ffn_shared_up_w"], a["L0_ffn_shared_down_w"])]]
    small = np.stack([
        a["L0_attn_w_k_down"], a["L0_attn_w_v_down"],
        a["L0_attn_q_to_latent"].transpose(2, 0, 1).reshape(L, E),
        a["L0_attn_v_up"].reshape(H // 2, 2, L, D).transpose(2, 1, 0, 3).reshape(L, E)], 1)
    c = np.zeros((P, C_WIDTH), np.float32)
    c[:, C_IDENT:C_IDENT + P] = np.eye(P)
    c[:, C_EXPERT:C_EXPERT + NE] = np.arange(NE)
    c[:, C_STEP:C_STEP + 8] = P * np.arange(8)
    c[:, C_BEFORE:C_BEFORE + NE * NE] = P * np.tril(np.ones((NE, NE)), -1).reshape(-1)
    c[:, C_BLOCK:C_BLOCK + BLOCKS] = P * np.arange(BLOCKS)
    c[:, C_POW] = -0.5
    c[:, C_CAUSAL:C_CAUSAL + T] = np.where(np.arange(T)[None] <= np.arange(P)[:, None] % T, 0.0, -1e30)
    c[:, C_RANK:C_RANK + P] = np.triu(np.ones((P, P)), 1)
    return {
        "x": x[:, :, order],
        "xT": x.reshape(TILES, P, KC, P).transpose(0, 3, 2, 1),
        "ctx_k": ctx.reshape(TILES, 2, T, XKV, XD).transpose(1, 3, 4, 0, 2),
        "ctx_v": ctx,
        "w_q": rows(a["L0_attn_w_q"].T),
        "w_small": small,
        "w_out": rows(a["L0_attn_w_out"].T[:, order]),
        "w_ffn": np.stack(ffn),
        "router": rows(a["L0_ffn_router_w"][order]),
        "consts": c,
    }


def build_program(nc, shapes):
    args = [nc.dram_tensor(name, shape, dt, kind="ExternalInput").ap() for name, shape, dt in shapes]
    out = nc.dram_tensor("out", (TILES, P, E), F32, kind="ExternalOutput").ap()
    decoder_layer(nc, *args, out)


def kernel(**inputs):
    import numpy as np
    import concourse.bacc as bacc
    from concourse.bass_utils import run_bass_kernel_spmd

    nc = bacc.Bacc("TRN2", target_bir_lowering=False, num_devices=1)
    arrays = {k: np.ascontiguousarray(v) for k, v in decoder_layout(inputs).items()}
    build_program(nc, [(k, v.shape, mybir.dt.from_np(v.dtype)) for k, v in arrays.items()])
    r = run_bass_kernel_spmd(nc, [arrays], core_ids=[0])
    return natural_order(r.results[0]["out"].reshape(B, T, E))
```
